# Optimizing a Trainium2 kernel written in Bass

```python
import numpy as np
import jax
import jax.numpy as jnp

def _softmax(x, axis=-1):
    return jax.nn.softmax(x, axis=axis)

def _gelu(x):
    return jax.nn.gelu(x, approximate=True)

def _silu(x):
    return jax.nn.silu(x)

def _sigmoid(x):
    return jax.nn.sigmoid(x)

def _layernorm(x, axis=-1, eps=1e-05):
    m = jnp.mean(x, axis=axis, keepdims=True)
    v = jnp.var(x, axis=axis, keepdims=True)
    return (x - m) / jnp.sqrt(v + eps)

def _scatter_add(tgt, idx, src, axis=0):
    return tgt.at[idx].add(src)

def _segment_sum(src, seg, n):
    return jax.ops.segment_sum(src, seg, n)
kernel_name = 'mk_adj_preln_d2_adj_r2_8bfc2f'

def setup_inputs(seed: int=0):
    np.random.seed(seed)
    _w = jnp.asarray

    def _rec_inputs():
        import jax
        import jax.numpy as jnp
        _gk = jax.random.key(seed)
        x = -1.394e-06 + 0.9999 * jax.random.normal(jax.random.fold_in(_gk, 1), (32, 256, 256), jnp.float32)
        _a = jax.random.bernoulli(jax.random.fold_in(_gk, 2), 0.0625, (32, 256, 256))
        adj = _a.astype(jnp.int32)
        return (x, adj)
    x, adj = _rec_inputs()

    def _L0_gnn_setup():
        import jax, jax.numpy as jnp
        import numpy as np
        NEG_INF = -1000000000.0
        NEG_SLOPE = 0.2

        def gat_layer(x, mask, W, a_src, a_dst, bias, concat):
            B, N, _ = x.shape
            H, F = a_src.shape
            xl = (x @ W).reshape(B, N, H, F)
            asrc = jnp.einsum('bnhf,hf->bnh', xl, a_src)
            adst = jnp.einsum('bnhf,hf->bnh', xl, a_dst)
            e = jax.nn.leaky_relu(asrc[:, :, None, :] + adst[:, None, :, :], NEG_SLOPE)
            e = jnp.where(mask[..., None], e, NEG_INF)
            attn = jax.nn.softmax(e, axis=1)
            out = jnp.einsum('bsdh,bshf->bdhf', attn, xl)
            if concat:
                out = out.reshape(B, N, H * F)
            else:
                out = out.mean(axis=2)
            return out + bias
        key = jax.random.key(seed)
        ks = jax.random.split(key, 10)
        B, N, Din, Fh, H, Dout = (8, 512, 256, 128, 4, 256)
        s = 0.05
        return {'adj': jax.random.randint(ks[0], (B, N, N), 0, 2, dtype=jnp.int32), 'x': jax.random.normal(ks[1], (B, N, Din), dtype=jnp.float32), 'W1': jax.random.normal(ks[2], (Din, H * Fh), dtype=jnp.float32) * s, 'att_src1': jax.random.normal(ks[3], (H, Fh), dtype=jnp.float32) * s, 'att_dst1': jax.random.normal(ks[4], (H, Fh), dtype=jnp.float32) * s, 'b1': jax.random.normal(ks[5], (H * Fh,), dtype=jnp.float32) * s, 'W2': jax.random.normal(ks[6], (H * Fh, Dout), dtype=jnp.float32) * s, 'att_src2': jax.random.normal(ks[7], (1, Dout), dtype=jnp.float32) * s, 'att_dst2': jax.random.normal(ks[8], (1, Dout), dtype=jnp.float32) * s, 'b2': jax.random.normal(ks[9], (Dout,), dtype=jnp.float32) * s}
    _L0_gnn_all = _L0_gnn_setup()
    _L0_gnn_in = {k: v for k, v in _L0_gnn_all.items() if k in ('W1', 'att_src1', 'att_dst1', 'b1', 'W2', 'att_src2', 'att_dst2', 'b2')}
    del _L0_gnn_all

    def _L1_gnn_setup():
        import jax, jax.numpy as jnp
        import numpy as np
        ALPHA = 0.2
        K_NUM = 16
        NEG_INF = -9000000000000000.0
        key = jax.random.key(seed)
        k1, k2, k3, k4 = jax.random.split(key, 4)
        B, N, F_in, F_out = (4, 1024, 256, 256)
        h = jax.random.normal(k1, (B, N, F_in), dtype=jnp.float32)
        adj = jax.random.randint(k2, (B, N, N), 0, 2, dtype=jnp.int32)

        def xavier(k, shape, gain=1.414):
            fan_in, fan_out = (shape[0], shape[1])
            bound = gain * np.sqrt(6.0 / (fan_in + fan_out))
            return jax.random.uniform(k, shape, jnp.float32, -bound, bound)
        W = xavier(k3, (F_in, F_out))
        a = xavier(k4, (2 * F_out, 1))
        return {'h': h, 'adj': adj, 'W': W, 'a': a}
    _L1_gnn_all = _L1_gnn_setup()
    _L1_gnn_in = {k: v for k, v in _L1_gnn_all.items() if k in ('W', 'a')}
    del _L1_gnn_all
    return {'x': x, 'adj': adj, 'L0_gnn_W1': _L0_gnn_in['W1'], 'L0_gnn_att_src1': _L0_gnn_in['att_src1'], 'L0_gnn_att_dst1': _L0_gnn_in['att_dst1'], 'L0_gnn_b1': _L0_gnn_in['b1'], 'L0_gnn_W2': _L0_gnn_in['W2'], 'L0_gnn_att_src2': _L0_gnn_in['att_src2'], 'L0_gnn_att_dst2': _L0_gnn_in['att_dst2'], 'L0_gnn_b2': _L0_gnn_in['b2'], 'L1_gnn_W': _L1_gnn_in['W'], 'L1_gnn_a': _L1_gnn_in['a']}

def reference(x, adj, L0_gnn_W1, L0_gnn_att_src1, L0_gnn_att_dst1, L0_gnn_b1, L0_gnn_W2, L0_gnn_att_src2, L0_gnn_att_dst2, L0_gnn_b2, L1_gnn_W, L1_gnn_a):
    import jax
    import jax.numpy as jnp

    def _L0_gnn_ref(adj, x, W1, att_src1, att_dst1, b1, W2, att_src2, att_dst2, b2):
        import jax, jax.numpy as jnp
        import numpy as np
        NEG_INF = -1000000000.0
        NEG_SLOPE = 0.2

        def gat_layer(x, mask, W, a_src, a_dst, bias, concat):
            B, N, _ = x.shape
            H, F = a_src.shape
            xl = (x @ W).reshape(B, N, H, F)
            asrc = jnp.einsum('bnhf,hf->bnh', xl, a_src)
            adst = jnp.einsum('bnhf,hf->bnh', xl, a_dst)
            e = jax.nn.leaky_relu(asrc[:, :, None, :] + adst[:, None, :, :], NEG_SLOPE)
            e = jnp.where(mask[..., None], e, NEG_INF)
            attn = jax.nn.softmax(e, axis=1)
            out = jnp.einsum('bsdh,bshf->bdhf', attn, xl)
            if concat:
                out = out.reshape(B, N, H * F)
            else:
                out = out.mean(axis=2)
            return out + bias
        B, N, _ = adj.shape
        mask = (adj > 0) | jnp.eye(N, dtype=bool)[None]
        h = jax.nn.elu(gat_layer(x, mask, W1, att_src1, att_dst1, b1, concat=True))
        h = gat_layer(h, mask, W2, att_src2, att_dst2, b2, concat=False)
        return h

    def _L1_gnn_ref(h, adj, W, a):
        import jax, jax.numpy as jnp
        import numpy as np
        ALPHA = 0.2
        K_NUM = 16
        NEG_INF = -9000000000000000.0
        F_out = W.shape[1]
        Wh = jnp.einsum('bnf,fo->bno', h, W)
        a1, a2 = (a[:F_out, 0], a[F_out:, 0])
        e_src = Wh @ a1
        e_dst = Wh @ a2
        e = e_src[:, :, None] + e_dst[:, None, :]
        e = jnp.where(e > 0, e, ALPHA * e)
        e = jnp.where(adj > 0, e, NEG_INF)
        attention = jax.nn.softmax(e, axis=2)
        topk_vals = jax.lax.top_k(attention, K_NUM)[0]
        kth = topk_vals[:, :, -1:]
        attention = jnp.where(attention < kth, 0.0, attention)
        h_prime = jnp.einsum('bij,bjo->bio', attention, Wh)
        return jax.nn.elu(h_prime)
    h = jnp.maximum(_layernorm(x, axis=-1), 0.0)
    x = x + _L0_gnn_ref(adj, h, L0_gnn_W1, L0_gnn_att_src1, L0_gnn_att_dst1, L0_gnn_b1, L0_gnn_W2, L0_gnn_att_src2, L0_gnn_att_dst2, L0_gnn_b2)
    h = jnp.maximum(_layernorm(x, axis=-1), 0.0)
    x = x + _L1_gnn_ref(h, adj, L1_gnn_W, L1_gnn_a)
    return x

_drawn_inputs = setup_inputs


def setup_inputs(seed=0):
    import zlib

    import numpy as np

    out = dict(_drawn_inputs(seed))
    spreads = {}
    factors = {'L0_gnn_att_src1': 5.623,
     'L0_gnn_att_dst1': 24.431,
     'L0_gnn_att_src2': 8.0,
     'L0_gnn_att_dst2': 37.255}
    for name, (base, spread) in spreads.items():
        noise = np.random.default_rng([zlib.crc32(name.encode()), seed]).standard_normal(out[name].shape)
        drawn = base * np.exp(spread * noise) if base else spread * noise
        out[name] = jnp.asarray(drawn.astype(out[name].dtype))
    for name, factor in factors.items():
        out[name] = (out[name] * factor).astype(out[name].dtype)
    return out
```

```python
from contextlib import ExitStack

import concourse.bass as bass
from concourse import mybir

ALU = mybir.AluOpType
ACT = mybir.ActivationFunctionType
F32 = mybir.dt.float32
F32R = mybir.dt.float32r
BF16 = mybir.dt.bfloat16
I32 = mybir.dt.int32

P = 128
NEG = -9.0e15
SLOPE = 0.2
EPS = 1e-5
LOWEST = -3.0e38
STAGES = "ABCD"
LAG = {"A": 0, "B": 1, "C": 2, "D": 3}


class Batch:

    def __init__(self, j, k):
        self.j, self.k = j, k

    @property
    def slot(self):
        return self.k % 2

    @property
    def index(self):
        return self.k if self.j is None else self.j * 2 + self.k

    def count(self, before=0):
        return self.k + 1 - before if self.j is None else self.j * 2 + (self.k + 1 - before)

    def dma_count(self, before=0):
        n = (self.k - before) // 2 + 1
        return 16 * n if self.j is None else self.j * 16 + 16 * n


def wait(eng, sem, value):
    if isinstance(value, int) and value <= 0:
        return
    eng.wait_ge(sem, value)


def settle(eng, passed):
    eng.sem_inc(passed)


def gat_stack(nc, x, adj, w1, att_src1, att_dst1, b1, w2, att_src2, att_dst2, b2, w3, a3, out):
    NB, N, D = x.shape
    H, F = att_src1.shape
    NC = N // P
    KC = D // P
    D2 = w2.shape[1]
    D3 = w3.shape[1]
    TOP = 16
    LAST = NB - 1
    assert NC == 2 and KC == 2 and F == P and H == 4 and D2 == D3 == D == N == 2 * P and NB % 2 == 0

    with ExitStack() as ctx:
        def sb(name, shape, dt=F32):
            return ctx.enter_context(nc.sbuf_tensor(name, shape, dt))

        def sem(name):
            return ctx.enter_context(nc.semaphore(name))

        ident = sb("ident", [P, P])
        ident_bf = sb("ident_bf", [P, P], BF16)
        off_diag = sb("off_diag", [P, NC, N], BF16)
        minus_half = sb("minus_half", [P, NC])
        w1_sb = sb("w1_sb", [P, KC, H * F])
        w2_sb = sb("w2_sb", [P, H, D2 + 2])
        w3_sb = sb("w3_sb", [P, KC, D3 + 2])
        wab1 = sb("wab1", [P, KC, 2 * H])
        att1 = sb("att1", [P, 2, H * F])
        att2 = sb("att2", [P, 2, D2])
        att3 = sb("att3", [P, 2, D3])
        b1_col = sb("b1_col", [P, H])
        b1_less1 = sb("b1_less1", [P, H])
        b2_row = sb("b2_row", [P, D2])
        prod = sb("prod", [P, D2])
        x_a = sb("x_a", [P, 2, NC, D])
        adj_a = sb("adj_a", [P, 2, NC, N], I32)
        bn_a = sb("bn_a", [P, NC, 6])
        mv_a = sb("mv_a", [P, NC, 2])
        nmean_a = sb("nmean_a", [P, NC])
        veps_a = sb("veps_a", [P, NC])
        rstd_a = sb("rstd_a", [P, NC])
        xn_a = sb("xn_a", [P, NC, D])
        hT_a = sb("hT_a", [P, KC, N])
        neg_a = sb("neg_a", [P, NC, N], BF16)
        negT = sb("negT", [P, 2, NC, N], BF16)
        parts_a = sb("parts_a", [P, NC, 2, P])
        terms_a = sb("terms_a", [P, 2, 2, N], F32R)
        xl = sb("xl", [P, 2, NC, H * F])
        e_b = sb("e_b", [P, 2, H, N])
        l_b = sb("l_b", [P, 2, H, N])
        max_b = sb("max_b", [P, 2, H])
        nmax_b = sb("nmax_b", [P, 2, H])
        nlk_b = sb("nlk_b", [P, 2, H])
        p_b = sb("p_b", [P, NC, H, N])
        pn_b = sb("pn_b", [P, NC, H, N])
        sum_b = sb("sum_b", [P, NC, H])
        inv_b = sb("inv_b", [P, NC, H])
        pT_b = sb("pT_b", [P, 2, NC, N])
        u_b = sb("u_b", [P, H, N])
        r_b = sb("r_b", [P, H, N])
        h1T = sb("h1T", [P, 2, H, N])
        x_c = sb("x_c", [P, 2, NC, D])
        xb_c = sb("xb_c", [P, NC, D])
        xl2 = sb("xl2", [P, NC, D2 + 2])
        parts_c = sb("parts_c", [P, NC, 2, P])
        terms_c = sb("terms_c", [P, 2, N], F32R)
        e_c = sb("e_c", [P, NC, N])
        l_c = sb("l_c", [P, NC, N])
        max_c = sb("max_c", [P, NC])
        nmax_c = sb("nmax_c", [P, NC])
        nlk_c = sb("nlk_c", [P, NC])
        p_c = sb("p_c", [P, NC, N])
        sum_c = sb("sum_c", [P, NC])
        inv_c = sb("inv_c", [P, NC])
        pT_c = sb("pT_c", [P, NC, N])
        y = sb("y", [P, 2, NC, D])
        adj_d = sb("adj_d", [P, 2, NC, N], I32)
        bn_d = sb("bn_d", [P, NC, 6])
        mv_d = sb("mv_d", [P, NC, 2])
        nmean_d = sb("nmean_d", [P, NC])
        veps_d = sb("veps_d", [P, NC])
        rstd_d = sb("rstd_d", [P, NC])
        xn_d = sb("xn_d", [P, NC, D])
        hT_d = sb("hT_d", [P, KC, N])
        neg_d = sb("neg_d", [P, NC, N], BF16)
        wh = sb("wh", [P, NC, D3 + 2])
        parts_d = sb("parts_d", [P, NC, 2, P])
        terms_d = sb("terms_d", [P, 2, N], F32R)
        e_d = sb("e_d", [P, NC, N])
        l_d = sb("l_d", [P, NC, N])
        max_d = sb("max_d", [P, NC])
        nmax_d = sb("nmax_d", [P, NC])
        nlk_d = sb("nlk_d", [P, NC])
        p_d = sb("p_d", [P, NC, N])
        sum_d = sb("sum_d", [P, NC])
        inv_d = sb("inv_d", [P, NC])
        top_d = sb("top_d", [P, NC, TOP])
        rest_d = sb("rest_d", [P, NC, N])
        kept_d = sb("kept_d", [P, NC, N])
        pT_d = sb("pT_d", [P, NC, N])
        u_d = sb("u_d", [P, NC, D3])
        r_d = sb("r_d", [P, NC, D3])
        elu_d = sb("elu_d", [P, NC, D3])
        yless1 = sb("yless1", [P, NC, D])
        out_sb = sb("out_sb", [P, NC, D])

        bank_x = [ctx.enter_context(nc.psum_tensor(f"bank_x{i}", [P, 512], F32)) for i in range(2)]
        bank_t = ctx.enter_context(nc.psum_tensor("bank_t", [P, 2, 512], F32))
        bank_p = [ctx.enter_context(nc.psum_tensor(f"bank_p{i}", [P, 512], F32)) for i in range(2)]
        bank_o = [ctx.enter_context(nc.psum_tensor(f"bank_o{i}", [P, 512], F32)) for i in range(2)]

        in_consts = sem("in_consts")
        in_x_a = [sem(f"in_x_a{i}") for i in range(2)]
        in_adj_a = [sem(f"in_adj_a{i}") for i in range(2)]
        in_x_c = [sem(f"in_x_c{i}") for i in range(2)]
        in_adj_d = [sem(f"in_adj_d{i}") for i in range(2)]
        stored = sem("stored")
        id_zero, id_done, od_done, half_done = sem("id_zero"), sem("id_done"), sem("od_done"), sem("half_done")
        idbf_done, parts_zero, parts_done = sem("idbf_done"), sem("parts_zero"), sem("parts_done")
        weights_done = sem("weights_done")
        dve_passed, pool_passed = sem("dve_passed"), sem("pool_passed")
        bn_a_done, mv_a_done, stats_a, rstd_a_done = sem("bn_a_done"), sem("mv_a_done"), sem("stats_a"), sem("rstd_a_done")
        xn_a_done, xnT_a_done, hT_a_done = sem("xn_a_done"), sem("xnT_a_done"), sem("hT_a_done")
        neg_a_done, negT_a_done, negT_done = sem("neg_a_done"), sem("negT_a_done"), sem("negT_done")
        ab_done, hi_a_done, parts_a_done, termsT_a_done, terms_a_done = (
            sem("ab_done"), sem("hi_a_done"), sem("parts_a_done"), sem("termsT_a_done"), sem("terms_a_done"))
        xl_mm = [sem(f"xl_mm{i}") for i in range(NC)]
        xl_done = [sem(f"xl_done{i}") for i in range(NC)]
        t_b_half = [sem(f"t_b_half{i}") for i in range(NC)]
        t_b_done = [sem(f"t_b_done{i}") for i in range(NC)]
        e_b_done = [sem(f"e_b_done{i}") for i in range(NC)]
        nmax_b_done = [sem(f"nmax_b_done{i}") for i in range(NC)]
        nlk_b_done = [sem(f"nlk_b_done{i}") for i in range(NC)]
        l_b_done = [sem(f"l_b_done{i}") for i in range(NC)]
        p_b_done = [sem(f"p_b_done{i}") for i in range(NC)]
        inv_b_done = [sem(f"inv_b_done{i}") for i in range(NC)]
        pn_b_done = [sem(f"pn_b_done{i}") for i in range(NC)]
        pT_b_mm = [sem(f"pT_b_mm{i}") for i in range(H)]
        pT_b_done = [sem(f"pT_b_done{i}") for i in range(H)]
        o_b_head = [sem(f"o_b_head{i}") for i in range(H)]
        o_b_done = [o_b_head[1], o_b_head[3]]
        u_b_done = [sem(f"u_b_done{i}") for i in range(2)]
        r_b_done = [sem(f"r_b_done{i}") for i in range(2)]
        h1_done = [sem(f"h1_done{i}") for i in range(2)]
        xb_done = sem("xb_done")
        xl2_mm = [sem(f"xl2_mm{i}") for i in range(NC)]
        xl2_done = [sem(f"xl2_done{i}") for i in range(NC)]
        hi_c_done, parts_c_done, termsT_c_done, terms_c_done = sem("hi_c_done"), sem("parts_c_done"), sem("termsT_c_done"), sem("terms_c_done")
        t_c_done, e_c_done, nmax_c_done, nlk_c_done, l_c_done, p_c_done = (
            sem("t_c_done"), sem("e_c_done"), sem("nmax_c_done"), sem("nlk_c_done"), sem("l_c_done"), sem("p_c_done"))
        inv_c_done, pT_c_mm, pT_c_done, o_c_done, y_done = (
            sem("inv_c_done"), sem("pT_c_mm"), sem("pT_c_done"), sem("o_c_done"), sem("y_done"))
        bn_d_done, mv_d_done, stats_d, rstd_d_done = sem("bn_d_done"), sem("mv_d_done"), sem("stats_d"), sem("rstd_d_done")
        xn_d_done, xnT_d_done, hT_d_done, neg_d_done = sem("xn_d_done"), sem("xnT_d_done"), sem("hT_d_done"), sem("neg_d_done")
        wh_mm = [sem(f"wh_mm{i}") for i in range(NC)]
        wh_done = [sem(f"wh_done{i}") for i in range(NC)]
        hi_d_done, parts_d_done, termsT_d_done, terms_d_done = sem("hi_d_done"), sem("parts_d_done"), sem("termsT_d_done"), sem("terms_d_done")
        t_d_done, e_d_done, nmax_d_done, nlk_d_done, l_d_done, p_d_done = (
            sem("t_d_done"), sem("e_d_done"), sem("nmax_d_done"), sem("nlk_d_done"), sem("l_d_done"), sem("p_d_done"))
        top8_done, rest_done, top16_done, kept_done = sem("top8_done"), sem("rest_done"), sem("top16_done"), sem("kept_done")
        inv_d_done, pT_d_mm, pT_d_done, o_d_done = sem("inv_d_done"), sem("pT_d_mm"), sem("pT_d_done"), sem("o_d_done")
        u_d_done, r_d_done, elu_done, yless1_done, out_done = sem("u_d_done"), sem("r_d_done"), sem("elu_done"), sem("yless1_done"), sem("out_done")

        USERS = {
            "x0": [("C", xl2_done[0]), ("D", wh_done[0]), ("A", xl_done[0])],
            "x1": [("C", xl2_done[1]), ("D", wh_done[1]), ("A", xl_done[1])],
            "t0": [("B", e_b_done[0]), ("B", e_b_done[1]), ("C", e_c_done)],
            "t1": [("B", e_b_done[0]), ("B", e_b_done[1]), ("D", e_d_done)],
            "p0": [("D", hT_d_done), ("D", terms_d_done), ("A", negT_done),
                   ("B", pT_b_done[0]), ("B", pT_b_done[2]), ("C", pT_c_done)],
            "p1": [("C", terms_c_done), ("A", hT_a_done), ("A", terms_a_done),
                   ("B", pT_b_done[1]), ("B", pT_b_done[3]), ("D", pT_d_done)],
            "o0": [("B", r_b_done[0]), ("C", y_done)],
            "o1": [("A", parts_a_done), ("B", r_b_done[1]), ("D", r_d_done)],
        }

        def bank_free(eng, step, bank, me):
            users = USERS[bank]
            at = [s for _, s in users].index(me)
            whole = all(step[g] for g in STAGES) and step["s"].j is not None
            for n in [(at - 1) % len(users)] if whole else range(len(users)):
                stage, read = users[n]
                before = 0 if n < at else 1
                b = Batch(step["s"].j, step["s"].k - LAG[stage])
                value = b.count(before)
                if isinstance(value, int):
                    value = min(value, NB)
                wait(eng, read, value)

        def run(eng, program):
            def step(j, s):
                on = {g: Batch(j, s - LAG[g]) if j is not None or 0 <= s - LAG[g] <= LAST else None
                      for g in STAGES}
                on["s"] = Batch(j, s)
                program(eng, on)

            first = LAG["D"] + 1
            for s in range(first):
                step(None, s)
            with eng.Fori(0, (NB - first) // 2) as j:
                step(j, first)
                step(j, first + 1)
            for s in range(NB, NB + LAG["D"]):
                step(None, s)

        block = ctx.enter_context(nc.Block())

        def rows(a, b):
            return a[b.index, :, :].rearrange("(c p) d -> p c d", p=P)

        def sync_step(sp, on):
            a, c, d = on["A"], on["C"], on["D"]
            if a:
                wait(sp, xn_a_done, a.count(2))
                sp.dma_start(x_a[:, a.slot], rows(x, a)).then_inc(in_x_a[a.slot], 16)
                wait(sp, neg_a_done, a.count(2))
                sp.dma_start(adj_a[:, a.slot], rows(adj, a)).then_inc(in_adj_a[a.slot], 16)
            if c:
                wait(sp, xb_done, c.count(2))
                sp.dma_start(x_c[:, c.slot], rows(x, c)).then_inc(in_x_c[c.slot], 16)
            if d:
                wait(sp, neg_d_done, d.count(1))
                sp.dma_start(adj_d[:, d.slot], rows(adj, d)).then_inc(in_adj_d[d.slot], 16)

        @block.sync
        def _(sp):
            sp.dma_start(w1_sb[:], w1.rearrange("(k p) n -> p k n", p=P)).then_inc(in_consts, 16)
            sp.dma_start(w2_sb[:, :, 0:D2], w2.rearrange("(k p) n -> p k n", p=P)).then_inc(in_consts, 16)
            sp.dma_start(w3_sb[:, :, 0:D3], w3.rearrange("(k p) n -> p k n", p=P)).then_inc(in_consts, 16)
            for n, v in enumerate((att_src1, att_dst1)):
                sp.dma_start(att1[:, n, :], v.rearrange("(o h) f -> o (h f)", o=1).to_broadcast([P, H * F])).then_inc(in_consts, 16)
            for n, v in enumerate((att_src2, att_dst2)):
                sp.dma_start(att2[:, n, :], v.to_broadcast([P, D2])).then_inc(in_consts, 16)
            for n, half in enumerate((1, 0)):
                sp.dma_start(att3[:, n, :], a3[half * D3:(half + 1) * D3, :].rearrange("d o -> o d").to_broadcast([P, D3])).then_inc(in_consts, 16)
            sp.dma_start(b2_row[:], b2.rearrange("(o d) -> o d", o=1).to_broadcast([P, D2])).then_inc(in_consts, 16)
            with nc.allow_non_contiguous_dma(reason="512 values, once"):
                sp.dma_start(b1_col[:], b1.rearrange("(h p) -> p h", p=P)).then_inc(in_consts, 16)
            run(sp, sync_step)

        CONSTS = 16 * 11

        def pool_step(pool, on):
            a, b, c, d = (on[g] for g in STAGES)

            def rstd(bt, stats, veps, rstd, done, nmean, xin, xn, xn_done, xn_read):
                pool.wait_ge(stats, bt.count())
                wait(pool, xn_done, bt.count(1))
                nc.gpsimd.tensor_tensor(rstd[:], veps[:], minus_half[:], ALU.pow).then_inc(done, 1)
                pool.wait_ge(done, bt.count())
                wait(pool, xn_read, bt.count(1))
                settle(pool, pool_passed)
                for n in range(NC):
                    last = nc.gpsimd.tensor_scalar(xn[:, n, :], xin[:, bt.slot, n, :], nmean[:, n:n + 1],
                                                   rstd[:, n:n + 1], ALU.add, ALU.mult)
                last.then_inc(xn_done, 1)

            def norm(n):
                pool.wait_ge(inv_b_done[n], b.count())
                wait(pool, pT_b_mm[H - 1], b.count(1))
                settle(pool, pool_passed)
                for h in range(H):
                    last = nc.gpsimd.tensor_scalar(pn_b[:, n, h, :], p_b[:, n, h, :], inv_b[:, n, h:h + 1], 1.0,
                                                   ALU.mult, ALU.mult)
                last.then_inc(pn_b_done[n], 1)

            if d:
                rstd(d, stats_d, veps_d, rstd_d, rstd_d_done, nmean_d, y, xn_d, xn_d_done, xnT_d_done)
                pool.wait_ge(in_adj_d[d.slot], d.dma_count())
                wait(pool, e_d_done, d.count(1))
                settle(pool, pool_passed)
                nc.gpsimd.tensor_scalar(neg_d[:], adj_d[:, d.slot], 0.0, NEG, ALU.is_le, ALU.mult).then_inc(neg_d_done, 1)
            if a:
                pool.wait_ge(in_x_a[a.slot], a.dma_count())
                rstd(a, stats_a, veps_a, rstd_a, rstd_a_done, nmean_a, x_a, xn_a, xn_a_done, xnT_a_done)
            if b:
                norm(0)
            if c:
                pool.wait_ge(in_x_c[c.slot], c.dma_count())
                wait(pool, y_done, c.count(1))
                for n in range(NC):
                    last = nc.gpsimd.tensor_tensor(xb_c[:, n, :], x_c[:, c.slot, n, :], b2_row[:], ALU.add)
                last.then_inc(xb_done, 1)
            if b:
                norm(1)
            if d:
                wait(pool, out_done, d.count(1))
                settle(pool, pool_passed)
                nc.gpsimd.tensor_scalar(yless1[:], y[:, d.slot], -1.0, 1.0, ALU.add, ALU.mult).then_inc(yless1_done, 1)
                pool.wait_ge(yless1_done, d.count())
                pool.wait_ge(elu_done, d.count())
                wait(pool, stored, d.count(1) * 16)
                nc.gpsimd.tensor_tensor(out_sb[:], elu_d[:], yless1[:], ALU.add).then_inc(out_done, 1)
                pool.wait_ge(out_done, d.count())
                pool.dma_start(rows(out, d), out_sb[:]).then_inc(stored, 16)

        @block.gpsimd
        def _(pool):
            nc.gpsimd.memset(ident[:], 0.0)
            nc.gpsimd.memset(ident_bf[:], 0.0)
            nc.gpsimd.memset(minus_half[:], -0.5).then_inc(half_done, 1)
            nc.gpsimd.memset(off_diag[:], 1.0).then_inc(id_zero, 1)
            pool.wait_ge(id_zero, 1)
            for m in (ident, ident_bf):
                last = nc.gpsimd.affine_select(out=m[:], in_=m[:], compare_op=ALU.not_equal, fill=1.0, base=0,
                                               pattern=[[-1, P]], channel_multiplier=1)
            last.then_inc(id_done, 1)
            nc.gpsimd.affine_select(out=off_diag[:], in_=off_diag[:], compare_op=ALU.not_equal, fill=0.0, base=0,
                                    pattern=[[P, NC], [-1, N]], channel_multiplier=1).then_inc(od_done, 1)
            pool.wait_ge(half_done, 1)
            pool.wait_ge(in_consts, CONSTS)
            run(pool, pool_step)
            pool.wait_ge(stored, 16 * NB)

        def act_step(act, on):
            a, b, c, d = (on[g] for g in STAGES)

            def exps(n):
                act.wait_ge(l_b_done[n], b.count())
                wait(act, pn_b_done[n], b.count(1))
                for h in range(H):
                    last = nc.scalar.activation(p_b[:, n, h, :], l_b[:, n, h, :], ACT.Exp, bias=nlk_b[:, n, h:h + 1],
                                                accum_out=sum_b[:, n, h:h + 1])
                last.then_inc(p_b_done[n], 1)

            if c:
                for n in range(NC):
                    act.wait_ge(xl2_mm[n], c.count())
                    wait(act, o_c_done, c.count(1))
                    wait(act, parts_c_done, c.count(1))
                    nc.scalar.activation(xl2[:, n, :], bank_x[n][:, 0:D2 + 2], ACT.Copy).then_inc(xl2_done[n], 1)
            if b:
                exps(0)
            if d:
                act.wait_ge(xnT_d_done, d.count())
                wait(act, wh_mm[1], d.count(1))
                nc.scalar.activation(hT_d[:].rearrange("p k n -> p (k n)"), bank_p[0][:], ACT.Relu).then_inc(hT_d_done, 1)
            if c:
                act.wait_ge(termsT_c_done, c.count())
                wait(act, t_c_done, c.count(1))
                nc.scalar.activation(terms_c[:].rearrange("p g n -> p (g n)"), bank_p[1][:], ACT.Copy).then_inc(terms_c_done, 1)
            if d:
                for n in range(NC):
                    act.wait_ge(wh_mm[n], d.count())
                    wait(act, o_d_done, d.count(1))
                    wait(act, parts_d_done, d.count(1))
                    nc.scalar.activation(wh[:, n, :], bank_x[n][:, 0:D3 + 2], ACT.Copy).then_inc(wh_done[n], 1)
            if b:
                exps(1)
            if d:
                act.wait_ge(termsT_d_done, d.count())
                wait(act, t_d_done, d.count(1))
                nc.scalar.activation(terms_d[:].rearrange("p g n -> p (g n)"), bank_p[0][:], ACT.Copy).then_inc(terms_d_done, 1)
            if a:
                act.wait_ge(xnT_a_done, a.count())
                wait(act, xl_mm[1], a.count(1))
                nc.scalar.activation(hT_a[:].rearrange("p k n -> p (k n)"), bank_p[1][:], ACT.Relu).then_inc(hT_a_done, 1)
            if c:
                act.wait_ge(l_c_done, c.count())
                wait(act, pT_c_mm, c.count(1))
                for n in range(NC):
                    last = nc.scalar.activation(p_c[:, n, :], l_c[:, n, :], ACT.Exp, bias=nlk_c[:, n:n + 1],
                                                accum_out=sum_c[:, n:n + 1])
                last.then_inc(p_c_done, 1)
            if d:
                act.wait_ge(l_d_done, d.count())
                wait(act, kept_done, d.count(1))
                for n in range(NC):
                    last = nc.scalar.activation(p_d[:, n, :], l_d[:, n, :], ACT.Exp, bias=nlk_d[:, n:n + 1],
                                                accum_out=sum_d[:, n:n + 1])
                last.then_inc(p_d_done, 1)
            if a:
                for n in range(NC):
                    act.wait_ge(xl_mm[n], a.count())
                    wait(act, o_b_done[1], a.count(2))
                    nc.scalar.activation(xl[:, a.slot, n, :], bank_x[n][:], ACT.Copy).then_inc(xl_done[n], 1)
                act.wait_ge(termsT_a_done, a.count())
                wait(act, t_b_done[1], a.count(2))
                nc.scalar.activation(terms_a[:, a.slot].rearrange("p g n -> p (g n)"), bank_p[1][:], ACT.Copy).then_inc(terms_a_done, 1)
            if b:
                for h in range(H):
                    act.wait_ge(pT_b_mm[h], b.count())
                    wait(act, o_b_head[(h - 2) % H], b.count(0 if h >= 2 else 1))
                    nc.scalar.activation(pT_b[:, h % 2].rearrange("p k n -> p (k n)"), bank_p[h % 2][:], ACT.Copy).then_inc(pT_b_done[h], 1)
                for g in range(2):
                    act.wait_ge(o_b_done[g], b.count())
                    wait(act, h1_done[g], b.count(1))
                    for h in (2 * g, 2 * g + 1):
                        last = nc.scalar.activation(u_b[:, h, :], bank_o[g][:, (h % 2) * N:(h % 2 + 1) * N], ACT.Exp,
                                                    bias=b1_col[:, h:h + 1])
                    last.then_inc(u_b_done[g], 1)
            if c:
                act.wait_ge(pT_c_mm, c.count())
                wait(act, o_c_done, c.count(1))
                nc.scalar.activation(pT_c[:].rearrange("p k n -> p (k n)"), bank_p[0][:], ACT.Copy).then_inc(pT_c_done, 1)
            if d:
                act.wait_ge(pT_d_mm, d.count())
                wait(act, o_d_done, d.count(1))
                nc.scalar.activation(pT_d[:].rearrange("p k n -> p (k n)"), bank_p[1][:], ACT.Copy).then_inc(pT_d_done, 1)
                act.wait_ge(o_d_done, d.count())
                act.wait_ge(inv_d_done, d.count())
                wait(act, elu_done, d.count(1))
                for n in range(NC):
                    last = nc.scalar.activation(u_d[:, n, :], bank_o[1][:, n * D3:(n + 1) * D3], ACT.Exp,
                                                scale=inv_d[:, n:n + 1])
                last.then_inc(u_d_done, 1)

        @block.scalar
        def _(act):
            act.wait_ge(in_consts, CONSTS)
            run(act, act_step)

        def dve_step(dve, on):
            a, b, c, d = (on[g] for g in STAGES)

            def bn(bt, xin, bn_t, mv, done):
                wait(dve, done, bt.count(1))
                for n in range(NC):
                    last = nc.vector.bn_stats(bn_t[:, n, :], xin[:, bt.slot, n, :])
                last.then_inc(done, 1)

            def aggr(bt, bn_t, mv, bn_done, done):
                dve.wait_ge(bn_done, bt.count())
                settle(dve, dve_passed)
                for n in range(NC):
                    last = nc.vector.bn_aggr(mv[:, n, :], bn_t[:, n, :])
                last.then_inc(done, 1)

            def stats(bt, mv, nmean, veps, mv_done, done, xn_done):
                dve.wait_ge(mv_done, bt.count())
                wait(dve, xn_done, bt.count(1))
                nc.vector.tensor_scalar(nmean[:], mv[:, :, 0], -1.0, None, ALU.mult)
                nc.vector.tensor_scalar(veps[:], mv[:, :, 1], EPS, None, ALU.add).then_inc(done, 1)

            def parts(bt, dst, col, row, hi_done, done, free, nh):
                wait(dve, free, bt.count(1))
                g = dst[:].rearrange("p c g (h r) -> p c g h r", r=32)
                for v, k, r in ((col, 0, 0), (row, 1, 2)):
                    last = nc.vector.tensor_copy(g[:, :, k, 0:nh, r].bitcast(F32R), v)
                last.then_inc(hi_done, 1)
                dve.wait_ge(hi_done, bt.count())
                for v, k, r in ((col, 0, 0), (row, 1, 2)):
                    last = nc.vector.tensor_tensor(g[:, :, k, 0:nh, r + 1].bitcast(F32R), v, g[:, :, k, 0:nh, r], ALU.subtract)
                last.then_inc(done, 1)

            def ttr(n):
                dve.wait_ge(t_b_done[n], b.count())
                wait(dve, l_b_done[n], b.count(1))
                settle(dve, dve_passed)
                for h in range(H):
                    last = nc.vector.tensor_tensor_reduce(
                        e_b[:, n, h, :], bank_t[:, h % 2, (h // 2) * N:(h // 2 + 1) * N], negT[:, b.slot, n, :],
                        1.0, LOWEST, ALU.add, ALU.max, max_b[:, n, h:h + 1])
                last.then_inc(e_b_done[n], 1)

            def nmax(n):
                dve.wait_ge(e_b_done[n], b.count())
                nc.vector.tensor_scalar(nmax_b[:, n, :], max_b[:, n, :], -1.0, None, ALU.mult).then_inc(nmax_b_done[n], 1)

            def leaky(n):
                wait(dve, p_b_done[n], b.count(1))
                nc.vector.scalar_tensor_tensor(l_b[:, n], e_b[:, n], SLOPE, e_b[:, n], ALU.mult, ALU.max)
                dve.wait_ge(nmax_b_done[n], b.count())
                nc.vector.scalar_tensor_tensor(nlk_b[:, n, :], max_b[:, n, :], -SLOPE, nmax_b[:, n, :], ALU.mult,
                                               ALU.min).then_inc(l_b_done[n], 1)

            def recip(n):
                dve.wait_ge(p_b_done[n], b.count())
                wait(dve, pn_b_done[n], b.count(1))
                nc.vector.reciprocal(inv_b[:, n, :], sum_b[:, n, :]).then_inc(inv_b_done[n], 1)

            def scores(bt, bank, mask, e_t, mx, nmx, nlk, l_t, t_done, e_done, nmax_done, l_done, p_done):
                dve.wait_ge(t_done, bt.count())
                wait(dve, l_done, bt.count(1))
                settle(dve, dve_passed)
                for n in range(NC):
                    last = nc.vector.tensor_tensor_reduce(e_t[:, n, :], bank_t[:, bank, n * N:(n + 1) * N], mask[:, n, :],
                                                          1.0, LOWEST, ALU.add, ALU.max, mx[:, n:n + 1])
                last.then_inc(e_done, 1)
                dve.wait_ge(e_done, bt.count())
                nc.vector.tensor_scalar(nmx[:], mx[:], -1.0, None, ALU.mult).then_inc(nmax_done, 1)
                wait(dve, p_done, bt.count(1))
                nc.vector.scalar_tensor_tensor(l_t[:], e_t[:], SLOPE, e_t[:], ALU.mult, ALU.max)
                dve.wait_ge(nmax_done, bt.count())
                nc.vector.scalar_tensor_tensor(nlk[:], mx[:], -SLOPE, nmx[:], ALU.mult, ALU.min).then_inc(l_done, 1)

            def elu_b(g):
                dve.wait_ge(u_b_done[g], b.count())
                wait(dve, h1_done[g], b.count(1))
                for h in (2 * g, 2 * g + 1):
                    last = nc.vector.tensor_scalar(r_b[:, h, :], bank_o[g][:, (h % 2) * N:(h % 2 + 1) * N],
                                                   b1_less1[:, h:h + 1], -1.0, ALU.add, ALU.max)
                last.then_inc(r_b_done[g], 1)
                dve.wait_ge(r_b_done[g], b.count())
                wait(dve, xl2_mm[1], b.count(2))
                nc.vector.scalar_tensor_tensor(h1T[:, b.slot, 2 * g:2 * g + 2, :], u_b[:, 2 * g:2 * g + 2, :], 1.0,
                                               r_b[:, 2 * g:2 * g + 2, :], ALU.min, ALU.add).then_inc(h1_done[g], 1)

            if d:
                dve.wait_ge(y_done, d.count())
                bn(d, y, bn_d, mv_d, bn_d_done)
            if b:
                dve.wait_ge(negT_done, b.count())
                ttr(0)
            if d:
                aggr(d, bn_d, mv_d, bn_d_done, mv_d_done)
            if b:
                nmax(0)
            if d:
                stats(d, mv_d, nmean_d, veps_d, mv_d_done, stats_d, xn_d_done)
            if b:
                leaky(0)
            if c:
                dve.wait_ge(xl2_done[1], c.count())
                parts(c, parts_c, xl2[:, :, D2:D2 + 1], xl2[:, :, D2 + 1:D2 + 2], hi_c_done, parts_c_done, termsT_c_done, 1)
            if b:
                ttr(1)
                nmax(1)
                leaky(1)
            if a:
                dve.wait_ge(in_x_a[a.slot], a.dma_count())
                bn(a, x_a, bn_a, mv_a, bn_a_done)
                dve.wait_ge(in_adj_a[a.slot], a.dma_count())
                wait(dve, negT_a_done, a.count(1))
                nc.vector.tensor_scalar(neg_a[:], adj_a[:, a.slot], 0.0, NEG, ALU.is_le, ALU.mult).then_inc(neg_a_done, 1)
                aggr(a, bn_a, mv_a, bn_a_done, mv_a_done)
                stats(a, mv_a, nmean_a, veps_a, mv_a_done, stats_a, xn_a_done)
            if b:
                recip(0)
            if d:
                dve.wait_ge(wh_done[1], d.count())
                parts(d, parts_d, wh[:, :, D3:D3 + 1], wh[:, :, D3 + 1:D3 + 2], hi_d_done, parts_d_done, termsT_d_done, 1)
            if c:
                scores(c, 0, negT[:, c.slot], e_c, max_c, nmax_c, nlk_c, l_c, t_c_done, e_c_done, nmax_c_done, l_c_done, p_c_done)
            if b:
                recip(1)
            if d:
                dve.wait_ge(neg_d_done, d.count())
                scores(d, 1, neg_d, e_d, max_d, nmax_d, nlk_d, l_d, t_d_done, e_d_done, nmax_d_done, l_d_done, p_d_done)
            if a:
                dve.wait_ge(ab_done, a.count())
                ab = bank_o[1][:, 0:NC * 2 * H].rearrange("p (c g h) -> p c g h", c=NC, g=2)
                parts(a, parts_a, ab[:, :, 0, :], ab[:, :, 1, :], hi_a_done, parts_a_done, termsT_a_done, H)
                dve.wait_ge(negT_a_done, a.count())
                nc.vector.tensor_tensor(negT[:, a.slot].rearrange("p c n -> p (c n)"), bank_p[0][:].bitcast(BF16)[:, 0:NC * N],
                                        off_diag[:].rearrange("p c n -> p (c n)"), ALU.mult).then_inc(negT_done, 1)
            if d:
                dve.wait_ge(p_d_done, d.count())
                wait(dve, kept_done, d.count(1))
                settle(dve, dve_passed)
                for n in range(NC):
                    last = nc.vector.max(top_d[:, n, 0:8], p_d[:, n, :])
                last.then_inc(top8_done, 1)
                dve.wait_ge(top8_done, d.count())
                settle(dve, dve_passed)
                for n in range(NC):
                    last = nc.vector.match_replace(rest_d[:, n, :], top_d[:, n, 0:8], p_d[:, n, :], -1.0)
                last.then_inc(rest_done, 1)
                dve.wait_ge(rest_done, d.count())
                settle(dve, dve_passed)
                for n in range(NC):
                    last = nc.vector.max(top_d[:, n, 8:16], rest_d[:, n, :])
                last.then_inc(top16_done, 1)
                nc.vector.reciprocal(inv_d[:], sum_d[:]).then_inc(inv_d_done, 1)
                dve.wait_ge(top16_done, d.count())
                wait(dve, pT_d_mm, d.count(1))
                for n in range(NC):
                    last = nc.vector.scalar_tensor_tensor(kept_d[:, n, :], p_d[:, n, :], top_d[:, n, TOP - 1:TOP],
                                                          p_d[:, n, :], ALU.is_ge, ALU.mult)
                last.then_inc(kept_done, 1)
            if b:
                elu_b(0)
            if c:
                dve.wait_ge(p_c_done, c.count())
                nc.vector.reciprocal(inv_c[:], sum_c[:]).then_inc(inv_c_done, 1)
            if b:
                elu_b(1)
            if c:
                dve.wait_ge(o_c_done, c.count())
                dve.wait_ge(inv_c_done, c.count())
                dve.wait_ge(xb_done, c.count())
                wait(dve, yless1_done, c.count(2))
                for n in range(NC):
                    last = nc.vector.scalar_tensor_tensor(y[:, c.slot, n, :], bank_o[0][:, n * D2:(n + 1) * D2],
                                                          inv_c[:, n:n + 1], xb_c[:, n, :], ALU.mult, ALU.add)
                last.then_inc(y_done, 1)
            if d:
                dve.wait_ge(u_d_done, d.count())
                for n in range(NC):
                    last = nc.vector.tensor_scalar(r_d[:, n, :], bank_o[1][:, n * D3:(n + 1) * D3], inv_d[:, n:n + 1],
                                                   0.0, ALU.mult, ALU.max)
                last.then_inc(r_d_done, 1)
                dve.wait_ge(r_d_done, d.count())
                wait(dve, out_done, d.count(1))
                nc.vector.scalar_tensor_tensor(elu_d[:], u_d[:], 1.0, r_d[:], ALU.min, ALU.add).then_inc(elu_done, 1)

        @block.vector
        def _(dve):
            for t in (parts_a, parts_c, parts_d):
                last = nc.vector.memset(t[:], 0.0)
            last.then_inc(parts_zero, 1)
            dve.wait_ge(parts_zero, 1)
            for t in (parts_a, parts_c, parts_d):
                g = t[:].rearrange("p c g (h r) -> p c g h r", r=32)
                for k, r in ((0, 2), (0, 3), (1, 0), (1, 1)):
                    last = nc.vector.memset(g[:, :, k, :, r], 1.0)
            last.then_inc(parts_done, 1)
            dve.wait_ge(in_consts, CONSTS)
            n = 0

            def column(dst, w, att):
                nonlocal n
                nc.vector.tensor_tensor_reduce(prod[:, 0:w.shape[1]], w, att, 1.0, 0.0, ALU.mult, ALU.add,
                                               dst).then_inc(weights_done, 1)
                n += 1
                dve.wait_ge(weights_done, n)

            for k in range(KC):
                for g in range(2):
                    for h in range(H):
                        column(wab1[:, k, g * H + h:g * H + h + 1], w1_sb[:, k, h * F:(h + 1) * F], att1[:, g, h * F:(h + 1) * F])
                    column(w3_sb[:, k, D3 + g:D3 + g + 1], w3_sb[:, k, 0:D3], att3[:, g, :])
            for k in range(H):
                for g in range(2):
                    column(w2_sb[:, k, D2 + g:D2 + g + 1], w2_sb[:, k, 0:D2], att2[:, g, :])
            nc.vector.tensor_scalar(b1_less1[:], b1_col[:], -1.0, None, ALU.add).then_inc(weights_done, 1)
            dve.wait_ge(weights_done, n + 1)
            dve.wait_ge(od_done, 1)
            run(dve, dve_step)

        COLUMNS = KC * 2 * (H + 1) + H * 2 + 1

        def pe_step(pe, on):
            a, b, c, d = (on[g] for g in STAGES)

            def turn(dst, src, identity=ident):
                for k in range(2):
                    for n in range(2):
                        last = nc.tensor.transpose(dst[:, k, n * P:(n + 1) * P], src[:, n, k * P:(k + 1) * P], identity[:])
                return last

            def terms(bt, bank, me, src, ready, done):
                pe.wait_ge(ready, bt.count())
                bank_free(pe, on, f"p{bank}", me)
                dst = bank_p[bank][:].rearrange("p (g n) -> p g n", g=2)
                for n in range(NC):
                    for g in range(2):
                        last = nc.tensor.transpose(dst[:, g, n * P:(n + 1) * P], src[:, n, g, :], ident[:])
                last.then_inc(done, 1)

            def project(bt, lhsT, rhs, width, me, mm):
                for n in range(NC):
                    bank_free(pe, on, f"x{n}", me[n])
                    K = rhs.shape[1]
                    for k in range(K):
                        last = nc.tensor.matmul(bank_x[n][:, 0:width], lhsT[:, k, n * P:(n + 1) * P], rhs[:, k, :],
                                                start=(k == 0), stop=(k == K - 1))
                    last.then_inc(mm[n], 1)

            def t_b(n):
                if n == 0:
                    pe.wait_ge(terms_a_done, b.count())
                for g in range(2):
                    bank_free(pe, on, f"t{g}", e_b_done[n])
                for h in range(H):
                    if h == 2:
                        last.then_inc(t_b_half[n], 1)
                        pe.wait_ge(t_b_half[n], b.count())
                    r = slice(32 * h, 32 * h + 4)
                    last = nc.tensor.matmul(bank_t[:, h % 2, (h // 2) * N:(h // 2 + 1) * N],
                                            terms_a[r, b.slot, 1, n * P:(n + 1) * P], terms_a[r, b.slot, 0, :],
                                            start=True, stop=True)
                last.then_inc(t_b_done[n], 1)

            def t_one(bt, g, me, src, ready, done):
                pe.wait_ge(ready, bt.count())
                bank_free(pe, on, f"t{g}", me)
                for n in range(NC):
                    last = nc.tensor.matmul(bank_t[:, g, n * N:(n + 1) * N], src[0:4, 1, n * P:(n + 1) * P],
                                            src[0:4, 0, :], start=True, stop=True)
                last.then_inc(done, 1)

            def attend(bt, bank, me, pT, feats, ready, done):
                pe.wait_ge(ready, bt.count())
                bank_free(pe, on, f"o{bank}", me)
                for n in range(NC):
                    for k in range(NC):
                        last = nc.tensor.matmul(bank_o[bank][:, n * N:(n + 1) * N], pT[:, k, n * P:(n + 1) * P],
                                                feats[:, k, 0:D2], start=(k == 0), stop=(k == NC - 1))
                last.then_inc(done, 1)

            if c:
                pe.wait_ge(h1_done[1], c.count())
                project(c, h1T[:, c.slot], w2_sb, D2 + 2, xl2_done, xl2_mm)
            if b:
                t_b(0)
            if d:
                pe.wait_ge(xn_d_done, d.count())
                bank_free(pe, on, "p0", hT_d_done)
                turn(bank_p[0][:].rearrange("p (k n) -> p k n", k=KC), xn_d).then_inc(xnT_d_done, 1)
            if c:
                terms(c, 1, terms_c_done, parts_c, parts_c_done, termsT_c_done)
            if d:
                pe.wait_ge(hT_d_done, d.count())
                project(d, hT_d, w3_sb, D3 + 2, wh_done, wh_mm)
            if b:
                t_b(1)
            if c:
                t_one(c, 0, e_c_done, terms_c, terms_c_done, t_c_done)
            if d:
                terms(d, 0, terms_d_done, parts_d, parts_d_done, termsT_d_done)
            if a:
                pe.wait_ge(xn_a_done, a.count())
                bank_free(pe, on, "p1", hT_a_done)
                turn(bank_p[1][:].rearrange("p (k n) -> p k n", k=KC), xn_a).then_inc(xnT_a_done, 1)
                pe.wait_ge(neg_a_done, a.count())
            if d:
                t_one(d, 1, e_d_done, terms_d, terms_d_done, t_d_done)
            if a:
                bank_free(pe, on, "p0", negT_done)
                turn(bank_p[0][:].bitcast(BF16)[:, 0:NC * N].rearrange("p (k n) -> p k n", k=NC), neg_a,
                     ident_bf).then_inc(negT_a_done, 1)
                pe.wait_ge(hT_a_done, a.count())
                bank_free(pe, on, "o1", parts_a_done)
                for n in range(NC):
                    for k in range(KC):
                        last = nc.tensor.matmul(bank_o[1][:, n * 2 * H:(n + 1) * 2 * H], hT_a[:, k, n * P:(n + 1) * P],
                                                wab1[:, k, :], start=(k == 0), stop=(k == KC - 1))
                last.then_inc(ab_done, 1)
                project(a, hT_a, w1_sb, H * F, xl_done, xl_mm)
                terms(a, 1, terms_a_done, parts_a, parts_a_done, termsT_a_done)
            if b:
                for n in range(NC):
                    pe.wait_ge(pn_b_done[n], b.count())
                    pe.wait_ge(xl_done[n], b.count())
                for h in range(H + 1):
                    if h < H:
                        bank_free(pe, on, f"p{h % 2}", pT_b_done[h])
                        turn(bank_p[h % 2][:].rearrange("p (k n) -> p k n", k=NC), pn_b[:, :, h, :]).then_inc(pT_b_mm[h], 1)
                    if h >= 1:
                        q = h - 1
                        if q % 2 == 0:
                            bank_free(pe, on, f"o{q // 2}", r_b_done[q // 2])
                        pe.wait_ge(pT_b_done[q], b.count())
                        for k in range(NC):
                            last = nc.tensor.matmul(bank_o[q // 2][:, (q % 2) * N:(q % 2 + 1) * N],
                                                    xl[:, b.slot, k, q * F:(q + 1) * F], pT_b[:, q % 2, k, :],
                                                    start=(k == 0), stop=(k == NC - 1))
                        last.then_inc(o_b_head[q], 1)
            if c:
                pe.wait_ge(p_c_done, c.count())
                bank_free(pe, on, "p0", pT_c_done)
                turn(bank_p[0][:].rearrange("p (k n) -> p k n", k=NC), p_c).then_inc(pT_c_mm, 1)
            if d:
                pe.wait_ge(kept_done, d.count())
                bank_free(pe, on, "p1", pT_d_done)
                turn(bank_p[1][:].rearrange("p (k n) -> p k n", k=NC), kept_d).then_inc(pT_d_mm, 1)
            if c:
                attend(c, 0, y_done, pT_c, xl2, pT_c_done, o_c_done)
            if d:
                attend(d, 1, r_d_done, pT_d, wh, pT_d_done, o_d_done)

        @block.tensor
        def _(pe):
            pe.wait_ge(id_done, 1)
            pe.wait_ge(parts_done, 1)
            pe.wait_ge(in_consts, CONSTS)
            pe.wait_ge(weights_done, COLUMNS)
            run(pe, pe_step)


_INS = ["x", "adj", "L0_gnn_W1", "L0_gnn_att_src1", "L0_gnn_att_dst1", "L0_gnn_b1", "L0_gnn_W2",
        "L0_gnn_att_src2", "L0_gnn_att_dst2", "L0_gnn_b2", "L1_gnn_W", "L1_gnn_a"]


def kernel(**inputs):
    import numpy as _np
    import concourse.bacc as _bacc
    from concourse import mybir as _mybir
    from concourse.bass_utils import run_bass_kernel_spmd as _run

    nc = _bacc.Bacc("TRN2", target_bir_lowering=False, num_devices=1)
    arrays, args = {}, []
    for name in _INS:
        a = _np.ascontiguousarray(inputs[name])
        arrays[f"in_{name}"] = a
        args.append(nc.dram_tensor(f"in_{name}", a.shape, _mybir.dt.from_np(a.dtype), kind="ExternalInput").ap())
    shape = inputs["x"].shape
    args.append(nc.dram_tensor("out_x", shape, _mybir.dt.float32, kind="ExternalOutput").ap())
    gat_stack(nc, *args)
    r = _run(nc, [arrays], core_ids=[0])
    return r.results[0]["out_x"]
```

```python
from contextlib import ExitStack

import concourse.bass as bass
from concourse import mybir

ALU = mybir.AluOpType
ACT = mybir.ActivationFunctionType
F32 = mybir.dt.float32
F32R = mybir.dt.float32r
BF16 = mybir.dt.bfloat16
I32 = mybir.dt.int32

P = 128
NEG = -9.0e15
SLOPE = 0.2
EPS = 1e-5
LOWEST = -3.0e38

LAG = {
    "xnT_a": 0, "maskT_a": 0, "xl0": 0, "xl1": 0, "termsT_a": 0, "t0_b": 0, "t1_b": 0, "pT2_b": 0,
    "pT3_b": 0, "pT0_b": 0, "pT1_b": 0, "o0_b": 0,
    "o1_b": 1, "o2_b": 1, "o3_b": 1, "xl1_c": 1, "xl0_c": 1, "termsT_c": 1, "t_c": 1,
    "pT_c": 2, "o_c": 2, "xnT_d": 2, "wh1_d": 2, "wh0_d": 2, "termsT_d": 2,
    "t_d": 3, "pT_d": 3,
    "o_d": 4,
    "bn_a": 0, "aggr_a": 0, "stats_a": 0, "mask_a": 0, "parts_a": 0, "negT": 0, "e0_b": 0, "l0_b": 0,
    "e1_b": 0, "l1_b": 0, "inv0_b": 0, "inv1_b": 0,
    "h1_0_b": 1, "h1_1_b": 1, "parts_c": 1, "e_c": 1, "l_c": 1,
    "inv_c": 2, "y_c": 2, "bn_d": 2, "aggr_d": 2, "stats_d": 2, "parts_d": 2,
    "mask_d": 3, "e_d": 3, "l_d": 3, "top8_d": 3, "rest_d": 3, "top16_d": 3, "kept_d": 3,
    "relu_d": 4, "elu_d": 4,
    "hT_a": 0, "xl0_out": 0, "xl1_out": 0, "terms_a": 0, "p0_b": 0, "p1_b": 0, "pT2_out": 0,
    "pT3_out": 0, "pT0_out": 0, "pT1_out": 0,
    "u0_b": 1, "u1_b": 1, "xl1_c_out": 1, "xl0_c_out": 1, "terms_c": 1, "p_c": 1,
    "pT_c_out": 2, "hT_d": 2, "wh1_out": 2, "wh0_out": 2,
    "terms_d": 3, "p_d": 3, "pT_d_out": 3,
    "u_d": 4,
    "rstd_a": 0, "xn_a": 0, "norm0_b": 0, "norm1_b": 0,
    "xb_c": 2, "rstd_d": 2, "xn_d": 2,
    "yless1": 4, "add_d": 4,
    "load_x_a": 0, "load_adj_a": 0, "load_x_c": 2, "load_adj_d": 3, "store": 5,
}
MAX_LAG = max(LAG.values())

BANKS = {
    "o2_b": (3,), "xnT_a": (0,), "pT_c": (2,), "t_d": (4,), "maskT_a": (5,), "xl0": (0, 1),
    "xl1": (2, 3), "o_c": (1,), "termsT_a": (0,), "t0_b": (0, 1), "t1_b": (2, 3), "xl1_c": (4,),
    "xl0_c": (0,), "xnT_d": (1,), "o_d": (4,), "termsT_c": (0,), "wh1_d": (3,), "t_c": (0,),
    "wh0_d": (1,), "pT_d": (3,), "pT2_b": (0,), "pT3_b": (2,), "pT0_b": (3,), "pT1_b": (1,),
    "termsT_d": (4,), "o0_b": (0,),
}
USERS = {
    0: ["xnT_a", "xl0", "termsT_a", "t0_b", "xl0_c", "termsT_c", "t_c", "pT2_b", "o0_b"],
    1: ["xl0", "o_c", "t0_b", "xnT_d", "wh0_d", "pT1_b"],
    2: ["pT_c", "xl1", "t1_b", "pT3_b"],
    3: ["o2_b", "xl1", "t1_b", "wh1_d", "pT_d", "pT0_b"],
    4: ["t_d", "xl1_c", "o_d", "termsT_d"],
    5: ["maskT_a"],
}
HEADS_TURNED = (2, 3, 0, 1)
HEADS_SUMMED = (0, 1, 2, 3)
LAST_T = 1
LAST_XL = 1
LAST_XL2 = 0
LAST_WH = 0


class Batch:

    def __init__(self, j, k):
        self.j, self.k = j, k

    def of(self, ring):
        return ring[self.k % len(ring)]

    @property
    def index(self):
        return self.k if self.j is None else self.j * 2 + self.k

    def count(self, before=0):
        return self.k + 1 - before if self.j is None else self.j * 2 + (self.k + 1 - before)

    def dma_count(self, before=0):
        n = (self.k - before) // 2 + 1
        return 16 * n if self.j is None else self.j * 16 + 16 * n


def wait(eng, sem, value):
    if isinstance(value, int) and value <= 0:
        return
    eng.wait_ge(sem, value)


def settle(eng, passed):
    eng.sem_inc(passed)


def gat_stack(nc, x, adj, w1, att_src1, att_dst1, b1, w2, att_src2, att_dst2, b2, w3, a3, out):
    NB, N, D = x.shape
    H, F = att_src1.shape
    NC = N // P
    KC = D // P
    G = 2
    HG = H // G
    W1 = HG * F + 2 * HG
    D2 = w2.shape[1]
    D3 = w3.shape[1]
    TOP = 16
    LAST = NB - 1
    assert NC == 2 and KC == 2 and F == P and H == 4 and D2 == D3 == D == N == 2 * P and NB % 2 == 0

    with ExitStack() as ctx:
        def sb(name, shape, dt=F32):
            return ctx.enter_context(nc.sbuf_tensor(name, shape, dt))

        def ring(name, slots, shape, dt=F32):
            return [sb(f"{name}_{i}", shape, dt) for i in range(slots)]

        def sem(name):
            return ctx.enter_context(nc.semaphore(name))

        def sems(name, n):
            return [sem(f"{name}{i}") for i in range(n)]

        ident = sb("ident", [P, P])
        ident_bf = sb("ident_bf", [P, P], BF16)
        ones = sb("ones", [P, N])
        off_diag = sb("off_diag", [P, NC, N], BF16)
        minus_half = sb("minus_half", [P, NC])
        minus_one = sb("minus_one", [P, 1])
        w1_sb = sb("w1_sb", [P, KC, G, W1])
        w2_sb = sb("w2_sb", [P, H, D2 + 2])
        w3_sb = sb("w3_sb", [P, KC, D3 + 2])
        att1 = sb("att1", [P, 2, H * F])
        att2 = sb("att2", [P, 2, D2])
        att3 = sb("att3", [P, 2, D3])
        b1_two = sb("b1_two", [2, H * F])
        b1_hi = sb("b1_hi", [2, H * F], F32R)
        b1_lo = sb("b1_lo", [2, H * F])
        b1_hi_or_0 = sb("b1_hi_or_0", [2, H * F])
        b1_parts = sb("b1_parts", [2, H * F], F32R)
        ones_two = sb("ones_two", [2, N], F32R)
        b2_row = sb("b2_row", [P, D2])
        prod = sb("prod", [P, D2])
        w2_sums = sb("w2_sums", [P, D2 + 2])
        x_a = ring("x_a", 2, [P, NC, D])
        adj_a = ring("adj_a", 2, [P, NC, N], I32)
        bn_a = sb("bn_a", [P, NC, 6])
        mv_a = sb("mv_a", [P, NC, 2])
        nmean_a = sb("nmean_a", [P, NC])
        veps_a = sb("veps_a", [P, NC])
        rstd_a = sb("rstd_a", [P, NC])
        xn_a = ring("xn_a", 1, [P, NC, D])
        hT_a = ring("hT_a", 1, [P, KC, N])
        neg_a = ring("neg_a", 1, [P, NC, N], BF16)
        negT = ring("negT", 2, [P, NC, N], BF16)
        xl = ring("xl", 2, [P, NC, G, W1])
        parts_a = sb("parts_a", [P, NC, 2, P])
        terms_a = ring("terms_a", 1, [P, 2, N], F32R)
        e_b = sb("e_b", [P, NC, H, N])
        max_b = sb("max_b", [P, NC, H])
        nmax_b = sb("nmax_b", [P, NC, H])
        l_b = sb("l_b", [P, NC, H, N])
        nlk_b = sb("nlk_b", [P, NC, H])
        p_b = sb("p_b", [P, NC, H, N])
        sum_b = sb("sum_b", [P, NC, H])
        inv_b = sb("inv_b", [P, NC, H])
        pn_b = sb("pn_b", [P, NC, H, N])
        pT_b = sb("pT_b", [P, H, NC, N])
        u_b = sb("u_b", [P, G, HG * N])
        h1T = sb("h1T", [P, H, N])
        x_c = ring("x_c", 2, [P, NC, D])
        xb_c = ring("xb_c", 1, [P, NC, D])
        xl_c = ring("xl_c", 2, [P, NC, D2 + 2])
        parts_c = sb("parts_c", [P, NC, 2, P])
        terms_c = sb("terms_c", [P, 2, N], F32R)
        e_c = sb("e_c", [P, NC, N])
        max_c = sb("max_c", [P, NC])
        nmax_c = sb("nmax_c", [P, NC])
        l_c = sb("l_c", [P, NC, N])
        nlk_c = sb("nlk_c", [P, NC])
        p_c = sb("p_c", [P, NC, N])
        sum_c = sb("sum_c", [P, NC])
        inv_c = sb("inv_c", [P, NC])
        pT_c = sb("pT_c", [P, NC, N])
        y = ring("y", 2, [P, NC, D])
        adj_d = ring("adj_d", 2, [P, NC, N], I32)
        bn_d = sb("bn_d", [P, NC, 6])
        mv_d = sb("mv_d", [P, NC, 2])
        nmean_d = sb("nmean_d", [P, NC])
        veps_d = sb("veps_d", [P, NC])
        rstd_d = sb("rstd_d", [P, NC])
        xn_d = ring("xn_d", 1, [P, NC, D])
        hT_d = ring("hT_d", 1, [P, KC, N])
        neg_d = sb("neg_d", [P, NC, N], BF16)
        wh = ring("wh", 2, [P, NC, D3 + 2])
        parts_d = sb("parts_d", [P, NC, 2, P])
        terms_d = sb("terms_d", [P, 2, N], F32R)
        e_d = sb("e_d", [P, NC, N])
        max_d = sb("max_d", [P, NC])
        nmax_d = sb("nmax_d", [P, NC])
        l_d = sb("l_d", [P, NC, N])
        nlk_d = sb("nlk_d", [P, NC])
        p_d = sb("p_d", [P, NC, N])
        sum_d = sb("sum_d", [P, NC])
        inv_d = ring("inv_d", 2, [P, NC])
        top_d = sb("top_d", [P, NC, TOP])
        rest_d = sb("rest_d", [P, NC, N])
        kept_d = sb("kept_d", [P, NC, N])
        pT_d = sb("pT_d", [P, NC, N])
        u_d = sb("u_d", [P, NC, D3])
        r_d = sb("r_d", [P, NC, D3])
        elu_d = sb("elu_d", [P, NC, D3])
        yless1 = ring("yless1", 2, [P, NC, D])
        out_sb = ring("out_sb", 2, [P, NC, D])

        bank = ctx.enter_context(nc.psum_tensor("bank", [P, 8, 512], F32))

        def tile(op):
            return bank[:, BANKS[op][0], :]

        def halves(op):
            return tile(op).rearrange("p (g n) -> p g n", g=2)

        in_consts = sem("in_consts")
        in_x_a, in_adj_a, in_x_c, in_adj_d = sems("in_x_a", 2), sems("in_adj_a", 2), sems("in_x_c", 2), sems("in_adj_d", 2)
        stored = sems("stored", 2)
        id_zero, id_done, od_done, fills_done = sem("id_zero"), sem("id_done"), sem("od_done"), sem("fills_done")
        parts_zero, parts_done, weights_done = sem("parts_zero"), sem("parts_done"), sem("weights_done")
        w2_sums_mm = sem("w2_sums_mm")
        dve_passed, pool_passed = sem("dve_passed"), sem("pool_passed")
        bn_a_done, mv_a_done, stats_a_done, rstd_a_done = sem("bn_a_done"), sem("mv_a_done"), sem("stats_a_done"), sem("rstd_a_done")
        xn_a_done, xnT_a_done, hT_a_done = sem("xn_a_done"), sem("xnT_a_done"), sem("hT_a_done")
        neg_a_done, negT_a_done, negT_done = sem("neg_a_done"), sem("negT_a_done"), sem("negT_done")
        hi_a_done, parts_a_done, termsT_a_done, terms_a_done = (
            sem("hi_a_done"), sem("parts_a_done"), sem("termsT_a_done"), sem("terms_a_done"))
        xl_mm, xl_done = sems("xl_mm", NC), sems("xl_done", NC)
        t_b_half, t_b_done, e_b_done = sems("t_b_half", NC), sems("t_b_done", NC), sems("e_b_done", NC)
        nmax_b_done, l_b_done, p_b_done = sems("nmax_b_done", NC), sems("l_b_done", NC), sems("p_b_done", NC)
        inv_b_done, pn_b_done = sems("inv_b_done", NC), sems("pn_b_done", NC)
        pT_b_mm, pT_b_done, o_b_mm = sems("pT_b_mm", H), sems("pT_b_done", H), sems("o_b_mm", H)
        u_b_done, h1_done = sems("u_b_done", G), sems("h1_done", G)
        xb_c_done = sem("xb_c_done")
        xl_c_mm, xl_c_done = sems("xl_c_mm", NC), sems("xl_c_done", NC)
        hi_c_done, parts_c_done, termsT_c_done, terms_c_done = sem("hi_c_done"), sem("parts_c_done"), sem("termsT_c_done"), sem("terms_c_done")
        t_c_done, e_c_done, nmax_c_done, l_c_done, p_c_done = (
            sem("t_c_done"), sem("e_c_done"), sem("nmax_c_done"), sem("l_c_done"), sem("p_c_done"))
        inv_c_done, pT_c_mm, pT_c_done, o_c_done, y_done = (
            sem("inv_c_done"), sem("pT_c_mm"), sem("pT_c_done"), sem("o_c_done"), sem("y_done"))
        bn_d_done, mv_d_done, stats_d_done, rstd_d_done = sem("bn_d_done"), sem("mv_d_done"), sem("stats_d_done"), sem("rstd_d_done")
        xn_d_done, xnT_d_done, hT_d_done, neg_d_done = sem("xn_d_done"), sem("xnT_d_done"), sem("hT_d_done"), sem("neg_d_done")
        wh_mm, wh_done = sems("wh_mm", NC), sems("wh_done", NC)
        hi_d_done, parts_d_done, termsT_d_done, terms_d_done = sem("hi_d_done"), sem("parts_d_done"), sem("termsT_d_done"), sem("terms_d_done")
        t_d_done, e_d_done, nmax_d_done, l_d_done, p_d_done = (
            sem("t_d_done"), sem("e_d_done"), sem("nmax_d_done"), sem("l_d_done"), sem("p_d_done"))
        top8_done, rest_done, top16_done, kept_done = sem("top8_done"), sem("rest_done"), sem("top16_done"), sem("kept_done")
        inv_d_done, pT_d_mm, pT_d_done, o_d_done = sem("inv_d_done"), sem("pT_d_mm"), sem("pT_d_done"), sem("o_d_done")
        u_d_done, r_d_done, elu_done, yless1_done, out_done = sem("u_d_done"), sem("r_d_done"), sem("elu_done"), sem("yless1_done"), sem("out_done")

        READ = {
            "xnT_a": hT_a_done, "maskT_a": negT_done, "xl0": xl_done[0], "xl1": xl_done[1], "termsT_a": terms_a_done,
            "t0_b": e_b_done[0], "t1_b": e_b_done[1],
            "pT0_b": pT_b_done[0], "pT1_b": pT_b_done[1], "pT2_b": pT_b_done[2], "pT3_b": pT_b_done[3],
            "o0_b": h1_done[0], "o2_b": h1_done[1],
            "xl0_c": xl_c_done[0], "xl1_c": xl_c_done[1], "termsT_c": terms_c_done, "t_c": e_c_done, "pT_c": pT_c_done, "o_c": y_done,
            "xnT_d": hT_d_done, "wh0_d": wh_done[0], "wh1_d": wh_done[1], "termsT_d": terms_d_done, "t_d": e_d_done,
            "pT_d": pT_d_done, "o_d": r_d_done,
        }

        def bank_free(eng, b, op):
            step = b.k + LAG[op]
            for n in BANKS[op]:
                users = USERS[n]
                me = users.index(op)
                for other in [(me - 1) % len(users)] if b.j is not None else range(len(users)):
                    before = 0 if other < me else 1
                    value = Batch(b.j, step - LAG[users[other]]).count(before)
                    if isinstance(value, int):
                        value = min(value, NB)
                    wait(eng, READ[users[other]], value)

        FIRST = MAX_LAG + 2 + MAX_LAG % 2

        def run(eng, program):
            def step(j, s):
                def do(op, f, *args):
                    k = s - LAG[op]
                    if j is not None or 0 <= k <= LAST:
                        f(Batch(j, k), *args)
                program(do)

            for s in range(FIRST):
                step(None, s)
            with eng.Fori(0, (NB - FIRST) // 2) as j:
                step(j, FIRST)
                step(j, FIRST + 1)
            for s in range(NB, NB + MAX_LAG):
                step(None, s)

        CONSTS = 16 * 14
        W2_COLUMNS = H * 2
        WEIGHTS = W2_COLUMNS + KC * 2 * (H + 1) + 8

        block = ctx.enter_context(nc.Block())

        def rows(a, b):
            return a[b.index, :, :].rearrange("(c p) d -> p c d", p=P)

        @block.sync
        def _(sp):
            for g in range(G):
                for k in range(KC):
                    sp.dma_start(w1_sb[:, k, g, 0:HG * F], w1[k * P:(k + 1) * P, g * HG * F:(g + 1) * HG * F]).then_inc(in_consts, 16)
            sp.dma_start(w2_sb[:, :, 0:D2], w2.rearrange("(k p) n -> p k n", p=P)).then_inc(in_consts, 16)
            sp.dma_start(w3_sb[:, :, 0:D3], w3.rearrange("(k p) n -> p k n", p=P)).then_inc(in_consts, 16)
            for n, v in enumerate((att_src1, att_dst1)):
                sp.dma_start(att1[:, n, :], v.rearrange("(o h) f -> o (h f)", o=1).to_broadcast([P, H * F])).then_inc(in_consts, 16)
            for n, v in enumerate((att_src2, att_dst2)):
                sp.dma_start(att2[:, n, :], v.to_broadcast([P, D2])).then_inc(in_consts, 16)
            for n, half in enumerate((1, 0)):
                sp.dma_start(att3[:, n, :], a3[half * D3:(half + 1) * D3, :].rearrange("d o -> o d").to_broadcast([P, D3])).then_inc(in_consts, 16)
            sp.dma_start(b2_row[:], b2.rearrange("(o d) -> o d", o=1).to_broadcast([P, D2])).then_inc(in_consts, 16)
            sp.dma_start(b1_two[:], b1.rearrange("(o d) -> o d", o=1).to_broadcast([2, H * F])).then_inc(in_consts, 16)

            def load(b, dst, src, loaded, read):
                wait(sp, read, b.count(2))
                sp.dma_start(b.of(dst)[:], rows(src, b)).then_inc(b.of(loaded), 16)

            def store(b):
                sp.wait_ge(out_done, b.count())
                sp.dma_start(rows(out, b), b.of(out_sb)[:]).then_inc(b.of(stored), 16)

            def sp_step(do):
                do("load_x_a", load, x_a, x, in_x_a, xn_a_done)
                do("load_x_c", load, x_c, x, in_x_c, xb_c_done)
                do("load_adj_d", load, adj_d, adj, in_adj_d, neg_d_done)
                do("load_adj_a", load, adj_a, adj, in_adj_a, neg_a_done)
                do("store", store)

            run(sp, sp_step)
            for done in stored:
                sp.wait_ge(done, 16 * NB // 2)


        @block.gpsimd
        def _(pool):
            nc.gpsimd.memset(ident[:], 0.0)
            nc.gpsimd.memset(ident_bf[:], 0.0)
            nc.gpsimd.memset(off_diag[:], 1.0).then_inc(id_zero, 1)
            pool.wait_ge(id_zero, 1)
            for m in (ident, ident_bf):
                last = nc.gpsimd.affine_select(out=m[:], in_=m[:], compare_op=ALU.not_equal, fill=1.0, base=0,
                                               pattern=[[-1, P]], channel_multiplier=1)
            last.then_inc(id_done, 1)
            nc.gpsimd.affine_select(out=off_diag[:], in_=off_diag[:], compare_op=ALU.not_equal, fill=0.0, base=0,
                                    pattern=[[P, NC], [-1, N]], channel_multiplier=1).then_inc(od_done, 1)
            nc.gpsimd.memset(ones[:], 1.0)
            nc.gpsimd.memset(minus_one[:], -1.0)
            nc.gpsimd.memset(minus_half[:], -0.5).then_inc(fills_done, 1)
            pool.wait_ge(fills_done, 1)
            pool.wait_ge(weights_done, WEIGHTS)

            def rstd(b, veps, dst, stats_done, done, xn_done):
                pool.wait_ge(stats_done, b.count())
                wait(pool, xn_done, b.count(1))
                nc.gpsimd.tensor_tensor(dst[:], veps[:], minus_half[:], ALU.pow).then_inc(done, 1)

            def normalise(b, dst, src, nmean, scale, scale_done, done, turned):
                pool.wait_ge(scale_done, b.count())
                wait(pool, turned, b.count(len(dst)))
                settle(pool, pool_passed)
                for n in range(NC):
                    last = nc.gpsimd.tensor_scalar(b.of(dst)[:, n, :], b.of(src)[:, n, :], nmean[:, n:n + 1],
                                                   scale[:, n:n + 1], ALU.add, ALU.mult)
                last.then_inc(done, 1)

            def make_rstd_a(b):
                rstd(b, veps_a, rstd_a, stats_a_done, rstd_a_done, xn_a_done)

            def make_xn_a(b):
                pool.wait_ge(b.of(in_x_a), b.dma_count())
                normalise(b, xn_a, x_a, nmean_a, rstd_a, rstd_a_done, xn_a_done, xnT_a_done)

            def make_norm_b(b, n):
                pool.wait_ge(inv_b_done[n], b.count())
                wait(pool, pT_b_mm[HEADS_TURNED[-1]], b.count(1))
                settle(pool, pool_passed)
                for h in range(H):
                    last = nc.gpsimd.tensor_scalar(pn_b[:, n, h, :], p_b[:, n, h, :], inv_b[:, n, h:h + 1], 1.0,
                                                   ALU.mult, ALU.mult)
                last.then_inc(pn_b_done[n], 1)

            def make_xb_c(b):
                pool.wait_ge(b.of(in_x_c), b.dma_count())
                wait(pool, y_done, b.count(len(xb_c)))
                for n in range(NC):
                    last = nc.gpsimd.tensor_tensor(b.of(xb_c)[:, n, :], b.of(x_c)[:, n, :], b2_row[:], ALU.add)
                last.then_inc(xb_c_done, 1)

            def make_rstd_d(b):
                rstd(b, veps_d, rstd_d, stats_d_done, rstd_d_done, xn_d_done)

            def make_xn_d(b):
                normalise(b, xn_d, y, nmean_d, rstd_d, rstd_d_done, xn_d_done, xnT_d_done)

            def make_yless1_d(b):
                pool.wait_ge(y_done, b.count())
                wait(pool, out_done, b.count(len(yless1)))
                settle(pool, pool_passed)
                nc.gpsimd.tensor_scalar(b.of(yless1)[:], b.of(y)[:], -1.0, 1.0, ALU.add, ALU.mult).then_inc(yless1_done, 1)

            def make_add_d(b):
                pool.wait_ge(yless1_done, b.count())
                pool.wait_ge(elu_done, b.count())
                if b.j is not None or b.k >= 2:
                    pool.wait_ge(b.of(stored), b.dma_count(2))
                nc.gpsimd.tensor_tensor(b.of(out_sb)[:], elu_d[:], b.of(yless1)[:], ALU.add).then_inc(out_done, 1)

            def pool_step(do):
                do("rstd_a", make_rstd_a)
                do("xn_a", make_xn_a)
                do("yless1", make_yless1_d)
                do("xb_c", make_xb_c)
                do("rstd_d", make_rstd_d)
                do("xn_d", make_xn_d)
                do("norm0_b", make_norm_b, 0)
                do("norm1_b", make_norm_b, 1)
                do("add_d", make_add_d)

            run(pool, pool_step)

        @block.scalar
        def _(act):
            act.wait_ge(fills_done, 1)
            act.wait_ge(weights_done, WEIGHTS)

            def evacuate(b, dst, src, done, ready, read, slots, func=ACT.Copy):
                act.wait_ge(ready, b.count())
                wait(act, read, b.count(slots))
                nc.scalar.activation(dst, src, func).then_inc(done, 1)

            def exps(b, dst, src, bias, sums, ready, read, done):
                act.wait_ge(ready, b.count())
                wait(act, read, b.count(1))
                for i in range(src.shape[1]):
                    last = nc.scalar.activation(dst[:, i, :], src[:, i, :], ACT.Exp, bias=bias[:, i:i + 1],
                                                accum_out=sums[:, i:i + 1])
                last.then_inc(done, 1)

            def make_hT_a(b):
                evacuate(b, b.of(hT_a)[:], halves("xnT_a"), hT_a_done, xnT_a_done, xl_mm[LAST_XL], len(hT_a), ACT.Relu)

            def make_xl_out(b, n):
                first = BANKS[f"xl{n}"][0]
                evacuate(b, b.of(xl)[:, n], bank[:, first:first + G, 0:W1], xl_done[n], xl_mm[n],
                         o_b_mm[HEADS_SUMMED[-1]], len(xl))

            def make_terms_a(b):
                evacuate(b, b.of(terms_a)[:], halves("termsT_a"), terms_a_done, termsT_a_done, t_b_done[LAST_T], len(terms_a))

            def make_p_b(b, n):
                exps(b, p_b[:, n], l_b[:, n], nlk_b[:, n], sum_b[:, n], l_b_done[n], pn_b_done[n], p_b_done[n])

            def make_pT_out(b, h):
                evacuate(b, pT_b[:, h], halves(f"pT{h}_b"), pT_b_done[h], pT_b_mm[h], o_b_mm[h], 1)

            def make_u_b(b, g):
                act.wait_ge(o_b_mm[HEADS_SUMMED[-1] if HEADS_SUMMED[-1] // HG == g else max(
                    range(g * HG, (g + 1) * HG), key=HEADS_SUMMED.index)], b.count())
                wait(act, h1_done[g], b.count(1))
                nc.scalar.activation(u_b[:, g], tile(f"o{g * HG}_b"), ACT.Exp, bias=minus_one[:]).then_inc(u_b_done[g], 1)

            def make_xl_c_out(b, n):
                evacuate(b, b.of(xl_c)[:, n], tile(f"xl{n}_c")[:, 0:D2 + 2], xl_c_done[n], xl_c_mm[n], o_c_done, len(xl_c))

            def make_terms_c(b):
                evacuate(b, terms_c[:], halves("termsT_c"), terms_c_done, termsT_c_done, t_c_done, 1)

            def make_p_c(b):
                exps(b, p_c, l_c, nlk_c, sum_c, l_c_done, pT_c_mm, p_c_done)

            def make_pT_c_out(b):
                evacuate(b, pT_c[:], halves("pT_c"), pT_c_done, pT_c_mm, o_c_done, 1)

            def make_hT_d(b):
                evacuate(b, b.of(hT_d)[:], halves("xnT_d"), hT_d_done, xnT_d_done, wh_mm[LAST_WH], len(hT_d), ACT.Relu)

            def make_wh_out(b, n):
                evacuate(b, b.of(wh)[:, n], tile(f"wh{n}_d")[:, 0:D3 + 2], wh_done[n], wh_mm[n], o_d_done, len(wh))

            def make_terms_d(b):
                evacuate(b, terms_d[:], halves("termsT_d"), terms_d_done, termsT_d_done, t_d_done, 1)

            def make_p_d(b):
                exps(b, p_d, l_d, nlk_d, sum_d, l_d_done, kept_done, p_d_done)

            def make_pT_d_out(b):
                evacuate(b, pT_d[:], halves("pT_d"), pT_d_done, pT_d_mm, o_d_done, 1)

            def make_u_d(b):
                act.wait_ge(o_d_done, b.count())
                act.wait_ge(inv_d_done, b.count())
                wait(act, elu_done, b.count(1))
                for n in range(NC):
                    last = nc.scalar.activation(u_d[:, n, :], halves("o_d")[:, n, :], ACT.Exp, scale=b.of(inv_d)[:, n:n + 1])
                last.then_inc(u_d_done, 1)

            def act_step(do):
                do("terms_d", make_terms_d)
                do("u0_b", make_u_b, 0)
                do("u1_b", make_u_b, 1)
                do("hT_a", make_hT_a)
                do("pT_c_out", make_pT_c_out)
                do("xl0_out", make_xl_out, 0)
                do("p_d", make_p_d)
                do("xl1_out", make_xl_out, 1)
                do("terms_a", make_terms_a)
                do("xl1_c_out", make_xl_c_out, 1)
                do("p0_b", make_p_b, 0)
                do("xl0_c_out", make_xl_c_out, 0)
                do("hT_d", make_hT_d)
                do("p1_b", make_p_b, 1)
                do("terms_c", make_terms_c)
                do("wh1_out", make_wh_out, 1)
                do("u_d", make_u_d)
                do("wh0_out", make_wh_out, 0)
                do("pT_d_out", make_pT_d_out)
                do("pT2_out", make_pT_out, 2)
                do("pT3_out", make_pT_out, 3)
                do("pT0_out", make_pT_out, 0)
                do("pT1_out", make_pT_out, 1)
                do("p_c", make_p_c)

            run(act, act_step)

        @block.vector
        def _(dve):
            for t in (parts_a, parts_c, parts_d):
                last = nc.vector.memset(t[:], 0.0)
            last.then_inc(parts_zero, 1)
            dve.wait_ge(parts_zero, 1)
            for t in (parts_a, parts_c, parts_d):
                g = t[:].rearrange("p c g (h r) -> p c g h r", r=32)
                for k, r in ((0, 2), (0, 3), (1, 0), (1, 1)):
                    last = nc.vector.memset(g[:, :, k, :, r], 1.0)
            last.then_inc(parts_done, 1)
            dve.wait_ge(in_consts, CONSTS)
            dve.wait_ge(fills_done, 1)
            dve.wait_ge(id_done, 1)
            dve.wait_ge(od_done, 1)
            made = 0

            def constant(instruction):
                nonlocal made
                instruction.then_inc(weights_done, 1)
                made += 1
                dve.wait_ge(weights_done, made)

            def column(dst, w, att):
                constant(nc.vector.tensor_tensor_reduce(prod[:, 0:w.shape[1]], w, att, 1.0, 0.0, ALU.mult, ALU.add, dst))

            for k in range(H):
                for g in range(2):
                    column(w2_sb[:, k, D2 + g:D2 + g + 1], w2_sb[:, k, 0:D2], att2[:, g, :])
            for k in range(KC):
                for g in range(2):
                    for h in range(H):
                        q, i = h // HG, h % HG
                        at = HG * F + g * HG + i
                        column(w1_sb[:, k, q, at:at + 1], w1_sb[:, k, q, i * F:(i + 1) * F], att1[:, g, h * F:(h + 1) * F])
                    column(w3_sb[:, k, D3 + g:D3 + g + 1], w3_sb[:, k, 0:D3], att3[:, g, :])
            constant(nc.vector.tensor_scalar(b1_two[:], b1_two[:], 1.0, None, ALU.add))
            constant(nc.vector.tensor_copy(b1_hi[:], b1_two[:]))
            constant(nc.vector.tensor_tensor(b1_lo[:], b1_two[:], b1_hi[:].bitcast(F32), ALU.subtract))
            constant(nc.vector.tensor_scalar(b1_hi_or_0[:], b1_hi[:].bitcast(F32), ident[0:2, 0:1], None, ALU.mult))
            constant(nc.vector.scalar_tensor_tensor(b1_parts[:], b1_lo[:], ident[0:2, 1:2], b1_hi_or_0[:], ALU.mult, ALU.add))
            constant(nc.vector.tensor_copy(ones_two[:], ones[0:2, :]))
            dve.wait_ge(w2_sums_mm, 1)
            constant(nc.vector.tensor_copy(w2_sums[:], bank[:, 0, 0:D2 + 2]))
            constant(nc.vector.tensor_tensor(b2_row[:], b2_row[:], w2_sums[:, 0:D2], ALU.subtract))

            def bn(b, xin, dst, done):
                wait(dve, done, b.count(1))
                for n in range(NC):
                    last = nc.vector.bn_stats(dst[:, n, :], b.of(xin)[:, n, :])
                last.then_inc(done, 1)

            def aggr(b, src, dst, src_done, done):
                dve.wait_ge(src_done, b.count())
                settle(dve, dve_passed)
                for n in range(NC):
                    last = nc.vector.bn_aggr(dst[:, n, :], src[:, n, :])
                last.then_inc(done, 1)

            def stats(b, mv, nmean, veps, mv_done, done, xn_done):
                dve.wait_ge(mv_done, b.count())
                wait(dve, xn_done, b.count(1))
                nc.vector.tensor_scalar(nmean[:], mv[:, :, 0], -1.0, None, ALU.mult)
                nc.vector.tensor_scalar(veps[:], mv[:, :, 1], EPS, None, ALU.add).then_inc(done, 1)

            def places(dst, heads):
                g = dst[:].rearrange("p c g (h r) -> p c g h r", r=32)
                return g[:, :, 0, 0:heads, 0], g[:, :, 1, 0:heads, 2], g[:, :, 0, 0:heads, 1], g[:, :, 1, 0:heads, 3]

            def scores(b, op, mask, e_t, mx, nmx, t_done, l_done, e_done):
                dve.wait_ge(t_done, b.count())
                wait(dve, l_done, b.count(1))
                settle(dve, dve_passed)
                for n in range(NC):
                    last = nc.vector.tensor_tensor_reduce(e_t[:, n, :], halves(op)[:, n, :], mask[:, n, :],
                                                          1.0, LOWEST, ALU.add, ALU.max, mx[:, n:n + 1])
                last.then_inc(e_done, 1)

            def leaky(b, e_t, mx, nmx, nlk, l_t, e_done, nmax_done, p_done, l_done):
                dve.wait_ge(e_done, b.count())
                nc.vector.tensor_scalar(nmx, mx, -1.0, None, ALU.mult).then_inc(nmax_done, 1)
                wait(dve, p_done, b.count(1))
                nc.vector.scalar_tensor_tensor(l_t, e_t, SLOPE, e_t, ALU.mult, ALU.max)
                dve.wait_ge(nmax_done, b.count())
                nc.vector.scalar_tensor_tensor(nlk, mx, -SLOPE, nmx, ALU.mult, ALU.min).then_inc(l_done, 1)

            def make_bn_a(b):
                dve.wait_ge(b.of(in_x_a), b.dma_count())
                bn(b, x_a, bn_a, bn_a_done)

            def make_aggr_a(b):
                aggr(b, bn_a, mv_a, bn_a_done, mv_a_done)

            def make_stats_a(b):
                stats(b, mv_a, nmean_a, veps_a, mv_a_done, stats_a_done, xn_a_done)

            def make_mask_a(b):
                dve.wait_ge(b.of(in_adj_a), b.dma_count())
                wait(dve, negT_a_done, b.count(len(neg_a)))
                nc.vector.tensor_scalar(b.of(neg_a)[:], b.of(adj_a)[:], 0.0, NEG, ALU.is_le, ALU.mult).then_inc(neg_a_done, 1)

            def make_negT(b):
                dve.wait_ge(negT_a_done, b.count())
                nc.vector.tensor_tensor(b.of(negT)[:].rearrange("p c n -> p (c n)"), tile("maskT_a").bitcast(BF16)[:, 0:NC * N],
                                        off_diag[:].rearrange("p c n -> p (c n)"), ALU.mult).then_inc(negT_done, 1)

            def make_parts_a(b):
                for n in range(NC):
                    dve.wait_ge(xl_done[n], b.count())
                wait(dve, termsT_a_done, b.count(1))
                hi_col, hi_row, lo_col, lo_row = [
                    t.rearrange("p c (q i) -> p c q i", q=G) for t in places(parts_a, H)]
                col, row = b.of(xl)[:, :, :, HG * F:HG * F + HG], b.of(xl)[:, :, :, HG * F + HG:W1]
                nc.vector.tensor_copy(hi_col.bitcast(F32R), col)
                nc.vector.tensor_copy(hi_row.bitcast(F32R), row).then_inc(hi_a_done, 1)
                dve.wait_ge(hi_a_done, b.count())
                nc.vector.tensor_tensor(lo_col.bitcast(F32R), col, hi_col, ALU.subtract)
                nc.vector.tensor_tensor(lo_row.bitcast(F32R), row, hi_row, ALU.subtract).then_inc(parts_a_done, 1)

            def make_e_b(b, n):
                dve.wait_ge(negT_done, b.count())
                dve.wait_ge(t_b_done[n], b.count())
                wait(dve, l_b_done[n], b.count(1))
                settle(dve, dve_passed)
                first = BANKS[f"t{n}_b"][0]
                for h in range(H):
                    last = nc.vector.tensor_tensor_reduce(
                        e_b[:, n, h, :], bank[:, first + h % 2, (h // 2) * N:(h // 2 + 1) * N], b.of(negT)[:, n, :],
                        1.0, LOWEST, ALU.add, ALU.max, max_b[:, n, h:h + 1])
                last.then_inc(e_b_done[n], 1)

            def make_l_b(b, n):
                leaky(b, e_b[:, n], max_b[:, n, :], nmax_b[:, n, :], nlk_b[:, n, :], l_b[:, n],
                      e_b_done[n], nmax_b_done[n], p_b_done[n], l_b_done[n])

            def make_inv_b(b, n):
                dve.wait_ge(p_b_done[n], b.count())
                wait(dve, pn_b_done[n], b.count(1))
                nc.vector.reciprocal(inv_b[:, n, :], sum_b[:, n, :]).then_inc(inv_b_done[n], 1)

            def make_h1_b(b, g):
                dve.wait_ge(u_b_done[g], b.count())
                wait(dve, xl_c_mm[LAST_XL2], b.count(1))
                nc.vector.scalar_tensor_tensor(h1T[:, g * HG:(g + 1) * HG, :].rearrange("p h n -> p (h n)"), u_b[:, g], 1.0,
                                               tile(f"o{g * HG}_b"), ALU.min, ALU.max).then_inc(h1_done[g], 1)

            def make_parts_c(b):
                for n in range(NC):
                    dve.wait_ge(xl_c_done[n], b.count())
                wait(dve, termsT_c_done, b.count(1))
                hi_col, hi_row, lo_col, lo_row = places(parts_c, 1)
                col, row = b.of(xl_c)[:, :, D2:D2 + 1], b.of(xl_c)[:, :, D2 + 1:D2 + 2]
                less_col, less_row = w2_sums[:, D2:D2 + 1], w2_sums[:, D2 + 1:D2 + 2]
                nc.vector.tensor_scalar(hi_col.bitcast(F32R), col, less_col, None, ALU.subtract)
                nc.vector.tensor_scalar(hi_row.bitcast(F32R), row, less_row, None, ALU.subtract).then_inc(hi_c_done, 1)
                dve.wait_ge(hi_c_done, b.count())
                nc.vector.scalar_tensor_tensor(lo_col.bitcast(F32R), col, less_col, hi_col, ALU.subtract, ALU.subtract)
                nc.vector.scalar_tensor_tensor(lo_row.bitcast(F32R), row, less_row, hi_row, ALU.subtract,
                                               ALU.subtract).then_inc(parts_c_done, 1)

            def make_e_c(b):
                dve.wait_ge(negT_done, b.count())
                scores(b, "t_c", b.of(negT), e_c, max_c, nmax_c, t_c_done, l_c_done, e_c_done)

            def make_l_c(b):
                leaky(b, e_c[:], max_c[:], nmax_c[:], nlk_c[:], l_c[:], e_c_done, nmax_c_done, p_c_done, l_c_done)

            def make_inv_c(b):
                dve.wait_ge(p_c_done, b.count())
                nc.vector.reciprocal(inv_c[:], sum_c[:]).then_inc(inv_c_done, 1)

            def make_y_c(b):
                dve.wait_ge(o_c_done, b.count())
                dve.wait_ge(inv_c_done, b.count())
                dve.wait_ge(xb_c_done, b.count())
                wait(dve, yless1_done, b.count(len(y)))
                for n in range(NC):
                    last = nc.vector.scalar_tensor_tensor(b.of(y)[:, n, :], halves("o_c")[:, n, :],
                                                          inv_c[:, n:n + 1], b.of(xb_c)[:, n, :], ALU.mult, ALU.add)
                last.then_inc(y_done, 1)

            def make_bn_d(b):
                dve.wait_ge(y_done, b.count())
                bn(b, y, bn_d, bn_d_done)

            def make_aggr_d(b):
                aggr(b, bn_d, mv_d, bn_d_done, mv_d_done)

            def make_stats_d(b):
                stats(b, mv_d, nmean_d, veps_d, mv_d_done, stats_d_done, xn_d_done)

            def make_mask_d(b):
                dve.wait_ge(b.of(in_adj_d), b.dma_count())
                wait(dve, e_d_done, b.count(1))
                nc.vector.tensor_scalar(neg_d[:], b.of(adj_d)[:], 0.0, NEG, ALU.is_le, ALU.mult).then_inc(neg_d_done, 1)

            def make_parts_d(b):
                for n in range(NC):
                    dve.wait_ge(wh_done[n], b.count())
                wait(dve, termsT_d_done, b.count(1))
                hi_col, hi_row, lo_col, lo_row = places(parts_d, 1)
                col, row = b.of(wh)[:, :, D3:D3 + 1], b.of(wh)[:, :, D3 + 1:D3 + 2]
                nc.vector.tensor_copy(hi_col.bitcast(F32R), col)
                nc.vector.tensor_copy(hi_row.bitcast(F32R), row).then_inc(hi_d_done, 1)
                dve.wait_ge(hi_d_done, b.count())
                nc.vector.tensor_tensor(lo_col.bitcast(F32R), col, hi_col, ALU.subtract)
                nc.vector.tensor_tensor(lo_row.bitcast(F32R), row, hi_row, ALU.subtract).then_inc(parts_d_done, 1)

            def make_e_d(b):
                dve.wait_ge(neg_d_done, b.count())
                scores(b, "t_d", neg_d, e_d, max_d, nmax_d, t_d_done, l_d_done, e_d_done)

            def make_l_d(b):
                leaky(b, e_d[:], max_d[:], nmax_d[:], nlk_d[:], l_d[:], e_d_done, nmax_d_done, p_d_done, l_d_done)

            def make_top8_d(b):
                dve.wait_ge(p_d_done, b.count())
                wait(dve, kept_done, b.count(1))
                settle(dve, dve_passed)
                for n in range(NC):
                    last = nc.vector.max(top_d[:, n, 0:8], p_d[:, n, :])
                last.then_inc(top8_done, 1)

            def make_rest_d(b):
                dve.wait_ge(top8_done, b.count())
                settle(dve, dve_passed)
                for n in range(NC):
                    last = nc.vector.match_replace(rest_d[:, n, :], top_d[:, n, 0:8], p_d[:, n, :], -1.0)
                last.then_inc(rest_done, 1)

            def make_top16_d(b):
                dve.wait_ge(rest_done, b.count())
                settle(dve, dve_passed)
                for n in range(NC):
                    last = nc.vector.max(top_d[:, n, 8:16], rest_d[:, n, :])
                last.then_inc(top16_done, 1)
                nc.vector.reciprocal(b.of(inv_d)[:], sum_d[:]).then_inc(inv_d_done, 1)

            def make_kept_d(b):
                dve.wait_ge(top16_done, b.count())
                wait(dve, pT_d_mm, b.count(1))
                for n in range(NC):
                    last = nc.vector.scalar_tensor_tensor(kept_d[:, n, :], p_d[:, n, :], top_d[:, n, TOP - 1:TOP],
                                                          p_d[:, n, :], ALU.is_ge, ALU.mult)
                last.then_inc(kept_done, 1)

            def make_relu_d(b):
                dve.wait_ge(u_d_done, b.count())
                for n in range(NC):
                    last = nc.vector.tensor_scalar(r_d[:, n, :], halves("o_d")[:, n, :], b.of(inv_d)[:, n:n + 1],
                                                   0.0, ALU.mult, ALU.max)
                last.then_inc(r_d_done, 1)

            def make_elu_d(b):
                dve.wait_ge(r_d_done, b.count())
                wait(dve, out_done, b.count(1))
                nc.vector.scalar_tensor_tensor(elu_d[:], u_d[:], 1.0, r_d[:], ALU.min, ALU.add).then_inc(elu_done, 1)

            def dve_step(do):
                do("bn_a", make_bn_a)
                do("inv_c", make_inv_c)
                do("aggr_a", make_aggr_a)
                do("stats_a", make_stats_a)
                do("h1_0_b", make_h1_b, 0)
                do("mask_a", make_mask_a)
                do("mask_d", make_mask_d)
                do("h1_1_b", make_h1_b, 1)
                do("e_d", make_e_d)
                do("l_d", make_l_d)
                do("top8_d", make_top8_d)
                do("parts_a", make_parts_a)
                do("negT", make_negT)
                do("y_c", make_y_c)
                do("bn_d", make_bn_d)
                do("aggr_d", make_aggr_d)
                do("e0_b", make_e_b, 0)
                do("stats_d", make_stats_d)
                do("l0_b", make_l_b, 0)
                do("e1_b", make_e_b, 1)
                do("l1_b", make_l_b, 1)
                do("inv0_b", make_inv_b, 0)
                do("parts_c", make_parts_c)
                do("rest_d", make_rest_d)
                do("top16_d", make_top16_d)
                do("inv1_b", make_inv_b, 1)
                do("kept_d", make_kept_d)
                do("e_c", make_e_c)
                do("l_c", make_l_c)
                do("parts_d", make_parts_d)
                do("relu_d", make_relu_d)
                do("elu_d", make_elu_d)

            run(dve, dve_step)

        @block.tensor
        def _(pe):
            pe.wait_ge(id_done, 1)
            pe.wait_ge(fills_done, 1)
            pe.wait_ge(parts_done, 1)
            pe.wait_ge(weights_done, W2_COLUMNS)
            for k in range(H):
                last = nc.tensor.matmul(bank[:, 0, 0:D2 + 2], ones[:, 0:P], w2_sb[:, k, :], start=(k == 0), stop=(k == H - 1))
            last.then_inc(w2_sums_mm, 1)
            pe.wait_ge(weights_done, WEIGHTS)

            def turn(dst, src, identity=ident):
                for k in range(2):
                    for n in range(2):
                        last = nc.tensor.transpose(dst[:, k, n * P:(n + 1) * P], src[:, n, k * P:(k + 1) * P], identity[:])
                return last

            def terms(b, op, src, ready, done):
                pe.wait_ge(ready, b.count())
                bank_free(pe, b, op)
                for n in range(NC):
                    for g in range(2):
                        last = nc.tensor.transpose(halves(op)[:, g, n * P:(n + 1) * P], src[:, n, g, :], ident[:])
                last.then_inc(done, 1)

            def project(dst, lhsT, rhs, n):
                K = rhs.shape[1]
                for k in range(K):
                    last = nc.tensor.matmul(dst, lhsT[:, k, n * P:(n + 1) * P], rhs[:, k], start=(k == 0), stop=(k == K - 1))
                return last

            def t_one(b, op, src, ready, done):
                pe.wait_ge(ready, b.count())
                bank_free(pe, b, op)
                for n in range(NC):
                    last = nc.tensor.matmul(halves(op)[:, n, :], src[0:4, 1, n * P:(n + 1) * P], src[0:4, 0, :],
                                            start=True, stop=True)
                last.then_inc(done, 1)

            def attend(b, op, pT, feats, ready, done):
                pe.wait_ge(ready, b.count())
                bank_free(pe, b, op)
                for n in range(NC):
                    for k in range(NC):
                        last = nc.tensor.matmul(halves(op)[:, n, :], pT[:, k, n * P:(n + 1) * P], feats[:, k, 0:D2],
                                                start=(k == 0), stop=(k == NC - 1))
                last.then_inc(done, 1)

            def make_xnT_a(b):
                pe.wait_ge(xn_a_done, b.count())
                bank_free(pe, b, "xnT_a")
                turn(halves("xnT_a"), b.of(xn_a)).then_inc(xnT_a_done, 1)

            def make_maskT_a(b):
                pe.wait_ge(neg_a_done, b.count())
                bank_free(pe, b, "maskT_a")
                turn(tile("maskT_a").bitcast(BF16)[:, 0:NC * N].rearrange("p (k n) -> p k n", k=NC), b.of(neg_a),
                     ident_bf).then_inc(negT_a_done, 1)

            def make_project_a(b, n):
                pe.wait_ge(hT_a_done, b.count())
                bank_free(pe, b, f"xl{n}")
                for g in range(G):
                    last = project(bank[:, BANKS[f"xl{n}"][g], 0:W1], b.of(hT_a), w1_sb[:, :, g, :], n)
                last.then_inc(xl_mm[n], 1)

            def make_termsT_a(b):
                terms(b, "termsT_a", parts_a, parts_a_done, termsT_a_done)

            def make_t_b(b, n):
                pe.wait_ge(terms_a_done, b.count())
                bank_free(pe, b, f"t{n}_b")
                first = BANKS[f"t{n}_b"][0]
                for h in range(H):
                    if h == 2:
                        last.then_inc(t_b_half[n], 1)
                        pe.wait_ge(t_b_half[n], b.count())
                    r = slice(32 * h, 32 * h + 4)
                    last = nc.tensor.matmul(bank[:, first + h % 2, (h // 2) * N:(h // 2 + 1) * N],
                                            b.of(terms_a)[r, 1, n * P:(n + 1) * P], b.of(terms_a)[r, 0, :],
                                            start=True, stop=True)
                last.then_inc(t_b_done[n], 1)

            def make_pT_b(b, h):
                for n in range(NC):
                    pe.wait_ge(pn_b_done[n], b.count())
                bank_free(pe, b, f"pT{h}_b")
                turn(halves(f"pT{h}_b"), pn_b[:, :, h, :]).then_inc(pT_b_mm[h], 1)

            def make_o_b(b, h):
                g, i = h // HG, h % HG
                if i == 0:
                    bank_free(pe, b, f"o{h}_b")
                dst = tile(f"o{g * HG}_b")[:, i * N:(i + 1) * N]
                pe.wait_ge(pT_b_done[h], b.count())
                for n in range(NC):
                    pe.wait_ge(xl_done[n], b.count())
                nc.tensor.matmul(dst, b1_parts[:, h * F:(h + 1) * F], ones_two[:], start=True, stop=False)
                for k in range(NC):
                    last = nc.tensor.matmul(dst, b.of(xl)[:, k, g, i * F:(i + 1) * F], pT_b[:, h, k, :],
                                            start=False, stop=(k == NC - 1))
                last.then_inc(o_b_mm[h], 1)

            def make_project_c(b, n):
                for g in range(G):
                    pe.wait_ge(h1_done[g], b.count())
                bank_free(pe, b, f"xl{n}_c")
                project(tile(f"xl{n}_c")[:, 0:D2 + 2], h1T, w2_sb, n).then_inc(xl_c_mm[n], 1)

            def make_termsT_c(b):
                terms(b, "termsT_c", parts_c, parts_c_done, termsT_c_done)

            def make_t_c(b):
                t_one(b, "t_c", terms_c, terms_c_done, t_c_done)

            def make_pT_c(b):
                pe.wait_ge(p_c_done, b.count())
                bank_free(pe, b, "pT_c")
                turn(halves("pT_c"), p_c).then_inc(pT_c_mm, 1)

            def make_o_c(b):
                attend(b, "o_c", pT_c, b.of(xl_c), pT_c_done, o_c_done)

            def make_xnT_d(b):
                pe.wait_ge(xn_d_done, b.count())
                bank_free(pe, b, "xnT_d")
                turn(halves("xnT_d"), b.of(xn_d)).then_inc(xnT_d_done, 1)

            def make_project_d(b, n):
                pe.wait_ge(hT_d_done, b.count())
                bank_free(pe, b, f"wh{n}_d")
                project(tile(f"wh{n}_d")[:, 0:D3 + 2], b.of(hT_d), w3_sb, n).then_inc(wh_mm[n], 1)

            def make_termsT_d(b):
                terms(b, "termsT_d", parts_d, parts_d_done, termsT_d_done)

            def make_t_d(b):
                t_one(b, "t_d", terms_d, terms_d_done, t_d_done)

            def make_pT_d(b):
                pe.wait_ge(kept_done, b.count())
                bank_free(pe, b, "pT_d")
                turn(halves("pT_d"), kept_d).then_inc(pT_d_mm, 1)

            def make_o_d(b):
                attend(b, "o_d", pT_d, b.of(wh), pT_d_done, o_d_done)

            def pe_step(do):
                do("o1_b", make_o_b, 1)
                do("o2_b", make_o_b, 2)
                do("o3_b", make_o_b, 3)
                do("xnT_a", make_xnT_a)
                do("pT_c", make_pT_c)
                do("t_d", make_t_d)
                do("maskT_a", make_maskT_a)
                do("xl0", make_project_a, 0)
                do("xl1", make_project_a, 1)
                do("o_c", make_o_c)
                do("termsT_a", make_termsT_a)
                do("t0_b", make_t_b, 0)
                do("t1_b", make_t_b, 1)
                do("xl1_c", make_project_c, 1)
                do("xl0_c", make_project_c, 0)
                do("xnT_d", make_xnT_d)
                do("o_d", make_o_d)
                do("termsT_c", make_termsT_c)
                do("wh1_d", make_project_d, 1)
                do("t_c", make_t_c)
                do("wh0_d", make_project_d, 0)
                do("pT_d", make_pT_d)
                do("pT2_b", make_pT_b, 2)
                do("pT3_b", make_pT_b, 3)
                do("pT0_b", make_pT_b, 0)
                do("pT1_b", make_pT_b, 1)
                do("termsT_d", make_termsT_d)
                do("o0_b", make_o_b, 0)

            run(pe, pe_step)


_INS = ["x", "adj", "L0_gnn_W1", "L0_gnn_att_src1", "L0_gnn_att_dst1", "L0_gnn_b1", "L0_gnn_W2",
        "L0_gnn_att_src2", "L0_gnn_att_dst2", "L0_gnn_b2", "L1_gnn_W", "L1_gnn_a"]


def kernel(**inputs):
    import numpy as _np
    import concourse.bacc as _bacc
    from concourse import mybir as _mybir
    from concourse.bass_utils import run_bass_kernel_spmd as _run

    nc = _bacc.Bacc("TRN2", target_bir_lowering=False, num_devices=1)
    arrays, args = {}, []
    for name in _INS:
        a = _np.ascontiguousarray(inputs[name])
        arrays[f"in_{name}"] = a
        args.append(nc.dram_tensor(f"in_{name}", a.shape, _mybir.dt.from_np(a.dtype), kind="ExternalInput").ap())
    shape = inputs["x"].shape
    args.append(nc.dram_tensor("out_x", shape, _mybir.dt.float32, kind="ExternalOutput").ap())
    gat_stack(nc, *args)
    r = _run(nc, [arrays], core_ids=[0])
    return r.results[0]["out_x"]
```

```python
from contextlib import ExitStack

import concourse.bass as bass
from concourse import mybir

ALU = mybir.AluOpType
ACT = mybir.ActivationFunctionType
F32 = mybir.dt.float32
F32R = mybir.dt.float32r
BF16 = mybir.dt.bfloat16
I32 = mybir.dt.int32

P = 128
NEG = -9.0e15
SLOPE = 0.2
EPS = 1e-5
LOWEST = -3.0e38

LAG = {
    "xnT_a": 0,
    "xl0": 1, "xl1": 1,
    "termsT_a": 2, "t_b": 2,
    "pT0_b": 3, "pT2_b": 3, "pT1_b": 3, "o0_b": 3, "o1_b": 3, "pT3_b": 3, "o2_b": 3, "o3_b": 3,
    "xl1_c": 3, "xl0_c": 3,
    "termsT_c": 4, "t_c": 4, "pT_c": 4, "o_c": 4,
    "xnT_d": 5, "wh1_d": 5, "wh0_d": 5, "termsT_d": 5,
    "t_d": 6, "pT_d": 6,
    "o_d": 7,
    "bn_a": 0, "aggr_a": 0, "stats_a": 0,
    "parts_a": 2, "negT": 2, "e0_b": 2, "e1_b": 2, "l1_b": 2, "l0_b": 2,
    "inv1_b": 3, "inv0_b": 3, "h1_0_b": 3, "h1_1_b": 3,
    "parts_c": 4, "e_c": 4, "l_c": 4,
    "inv_c": 5, "y_c": 5, "bn_d": 5, "aggr_d": 5, "stats_d": 5,
    "parts_d": 6, "mask_d": 6, "e_d": 6, "l_d": 6, "top8_d": 6, "rest_d": 6,
    "top16_d": 7, "kept_d": 7,
    "elu_d": 8,
    "hT_a": 1, "hT_hi_a": 1,
    "xl0_out": 2, "xl1_out": 2, "terms_a": 2,
    "p1_b": 3, "p0_b": 3, "pT0_out": 3, "pT2_out": 3, "pT1_out": 3, "u0_b": 3, "pT3_out": 3,
    "h1_hi0_b": 3, "u1_b": 3, "h1_hi1_b": 3,
    "xl1_c_out": 4, "xl0_c_out": 4, "terms_c": 4, "p_c": 4, "pT_c_out": 4,
    "hT_d": 5, "hT_hi_d": 5, "wh1_out": 5, "wh0_out": 5,
    "terms_d": 6, "p_d": 6,
    "pT_d_out": 7, "u_d": 7,
    "relu_d": 8,
    "rstd_a": 0, "xn_a": 0, "hT_lo_a": 0,
    "norm1_b": 2, "norm0_b": 2, "h1_lo0_b": 2,
    "h1_lo1_b": 3, "xb_c": 3,
    "rstd_d": 4, "xn_d": 4, "hT_lo_d": 4,
    "yless1": 6,
    "add_d": 7,
    "load_x_a": 0, "load_adjT_a": 1, "load_x_c": 2, "load_adj_d": 5, "store": 8,
}
MAX_LAG = max(LAG.values())

BANKS = {
    "t_d": (4,), "termsT_c": (6,), "pT0_b": (7,), "pT2_b": (0,), "pT1_b": (3,), "t_c": (5,),
    "o0_b": (2,), "termsT_a": (6,), "xnT_d": (0,), "pT3_b": (3,), "t_b": (6, 7, 4, 5), "o2_b": (1,),
    "o_d": (3,), "pT_c": (2,), "wh1_d": (0,), "wh0_d": (6,), "o_c": (2,), "xl0": (6, 7),
    "xl1_c": (0,), "xl0_c": (4,), "xnT_a": (1,), "termsT_d": (5,), "pT_d": (0,), "xl1": (2, 3),
}
USERS = {
    0: ["pT2_b", "xnT_d", "wh1_d", "xl1_c", "pT_d"],
    1: ["o2_b", "xnT_a"],
    2: ["o0_b", "pT_c", "o_c", "xl1"],
    3: ["pT1_b", "pT3_b", "o_d", "xl1"],
    4: ["t_d", "t_b", "xl0_c"],
    5: ["t_c", "t_b", "termsT_d"],
    6: ["termsT_c", "termsT_a", "t_b", "wh0_d", "xl0"],
    7: ["pT0_b", "t_b", "xl0"],
}
LAST_TURNED = 3
LAST_SUMMED = 3
LAST_XL = 1
LAST_XL2 = 0
LAST_WH = 0


class Batch:

    def __init__(self, j, k):
        self.j, self.k = j, k

    def of(self, ring):
        return ring[self.k % len(ring)]

    @property
    def index(self):
        return self.k if self.j is None else self.j * 2 + self.k

    def count(self, before=0):
        return self.k + 1 - before if self.j is None else self.j * 2 + (self.k + 1 - before)

    def dma_count(self, before=0):
        n = (self.k - before) // 2 + 1
        return 16 * n if self.j is None else self.j * 16 + 16 * n


def wait(eng, sem, value):
    if isinstance(value, int) and value <= 0:
        return
    eng.wait_ge(sem, value)


def settle(eng, passed):
    eng.sem_inc(passed)


def gat_stack(nc, x, adj, adj_turned, w1, att_src1, att_dst1, b1, w2, att_src2, att_dst2, b2, w3, a3, out):
    NB, N, D = x.shape
    H, F = att_src1.shape
    NC = N // P
    KC = D // P
    G = 2
    HG = H // G
    W1 = HG * F + 2 * HG
    D2 = w2.shape[1]
    D3 = w3.shape[1]
    TOP = 16
    LAST = NB - 1
    assert NC == 2 and KC == 2 and F == P and H == 4 and D2 == D3 == D == N == 2 * P and NB % 2 == 0

    with ExitStack() as ctx:
        def sb(name, shape, dt=F32):
            return ctx.enter_context(nc.sbuf_tensor(name, shape, dt))

        def ring(name, slots, shape, dt=F32):
            return [sb(f"{name}_{i}", shape, dt) for i in range(slots)]

        def sem(name):
            return ctx.enter_context(nc.semaphore(name))

        def sems(name, n):
            return [sem(f"{name}{i}") for i in range(n)]

        ident = sb("ident", [P, P])
        ident_r = sb("ident_r", [P, P], F32R)
        ones = sb("ones", [P, N])
        neg_off_diag = sb("neg_off_diag", [P, NC, N], BF16)
        minus_half = sb("minus_half", [P, NC])
        minus_one = sb("minus_one", [P, 1])
        w1_hi = sb("w1_hi", [P, KC, G, W1], F32R)
        w1_lo = sb("w1_lo", [P, KC, G, W1], F32R)
        w2_hi = sb("w2_hi", [P, H, D2 + 2], F32R)
        w2_lo = sb("w2_lo", [P, H, D2 + 2], F32R)
        w3_sb = sb("w3_sb", [P, KC, D3 + 2])
        w3_hi = sb("w3_hi", [P, KC, D3 + 2], F32R)
        w3_lo = sb("w3_lo", [P, KC, D3 + 2], F32R)
        att2 = sb("att2", [P, 2, D2])
        att3 = sb("att3", [P, 2, D3])
        b1_two = sb("b1_two", [2, H * F])
        b1_hi = sb("b1_hi", [2, H * F], F32R)
        b1_lo = sb("b1_lo", [2, H * F])
        b1_hi_or_0 = sb("b1_hi_or_0", [2, H * F])
        b1_parts = sb("b1_parts", [2, H * F], F32R)
        ones_two = sb("ones_two", [2, N], F32R)
        b2_row = sb("b2_row", [P, D2])
        prod = sb("prod", [P, D2])
        w2_sums = sb("w2_sums", [P, D2 + 2])
        x_a = ring("x_a", 2, [P, NC, D])
        adjT_a = ring("adjT_a", 2, [P, NC, N], I32)
        bn_a = sb("bn_a", [P, NC, 6])
        mv_a = sb("mv_a", [P, NC, 2])
        nmean_a = sb("nmean_a", [P, NC])
        veps_a = sb("veps_a", [P, NC])
        rstd_a = sb("rstd_a", [P, NC])
        xn_a = ring("xn_a", 1, [P, NC, D])
        hT_a = ring("hT_a", 1, [P, KC, N])
        hT_hi_a = ring("hT_hi_a", 1, [P, KC, N], F32R)
        hT_lo_a = ring("hT_lo_a", 1, [P, KC, N], F32R)
        negT = ring("negT", 2, [P, NC, N], BF16)
        xl = ring("xl", 2, [P, NC, G, W1])
        parts_a = sb("parts_a", [P, NC, 2, P], F32R)
        terms_a = ring("terms_a", 1, [P, 2, N], F32R)
        e_b = sb("e_b", [P, NC, H, N])
        max_b = sb("max_b", [P, NC, H])
        nmax_b = sb("nmax_b", [P, NC, H])
        l_b = sb("l_b", [P, NC, H, N])
        nlk_b = sb("nlk_b", [P, NC, H])
        p_b = sb("p_b", [P, NC, H, N])
        sum_b = sb("sum_b", [P, NC, H])
        inv_b = sb("inv_b", [P, NC, H])
        pn_b = sb("pn_b", [P, NC, H, N])
        pT_b = sb("pT_b", [P, H, NC, N])
        u_b = sb("u_b", [P, G, HG * N])
        h1T = sb("h1T", [P, H, N])
        h1T_hi = sb("h1T_hi", [P, H, N], F32R)
        h1T_lo = sb("h1T_lo", [P, H, N], F32R)
        early_l, early_pn = [t[:].rearrange("p c h n -> p (c h n)") for t in (l_b, pn_b)]
        early_pT = pT_b[:].rearrange("p h c n -> p (h c n)")
        w1_sb = early_l[:, 0:KC * G * W1].rearrange("p (k g n) -> p k g n", k=KC, g=G)
        w2_sb = early_pT[:, 0:H * (D2 + 2)].rearrange("p (h n) -> p h n", h=H)
        att1 = early_pn[:, 0:2 * H * F].rearrange("p (g n) -> p g n", g=2)
        x_c = ring("x_c", 2, [P, NC, D])
        xb_c = ring("xb_c", 1, [P, NC, D])
        xl_c = ring("xl_c", 2, [P, NC, D2 + 2])
        parts_c = sb("parts_c", [P, NC, 2, P], F32R)
        terms_c = sb("terms_c", [P, 2, N], F32R)
        e_c = sb("e_c", [P, NC, N])
        max_c = sb("max_c", [P, NC])
        nmax_c = sb("nmax_c", [P, NC])
        l_c = sb("l_c", [P, NC, N])
        nlk_c = sb("nlk_c", [P, NC])
        p_c = sb("p_c", [P, NC, N])
        sum_c = sb("sum_c", [P, NC])
        inv_c = sb("inv_c", [P, NC])
        pT_c = sb("pT_c", [P, NC, N])
        y = ring("y", 2, [P, NC, D])
        adj_d = ring("adj_d", 2, [P, NC, N], I32)
        bn_d = sb("bn_d", [P, NC, 6])
        mv_d = sb("mv_d", [P, NC, 2])
        nmean_d = sb("nmean_d", [P, NC])
        veps_d = sb("veps_d", [P, NC])
        rstd_d = sb("rstd_d", [P, NC])
        xn_d = ring("xn_d", 1, [P, NC, D])
        hT_d = ring("hT_d", 1, [P, KC, N])
        hT_hi_d = ring("hT_hi_d", 1, [P, KC, N], F32R)
        hT_lo_d = ring("hT_lo_d", 1, [P, KC, N], F32R)
        neg_d = sb("neg_d", [P, NC, N], BF16)
        wh = ring("wh", 2, [P, NC, D3 + 2])
        parts_d = sb("parts_d", [P, NC, 2, P], F32R)
        terms_d = sb("terms_d", [P, 2, N], F32R)
        e_d = sb("e_d", [P, NC, N])
        max_d = sb("max_d", [P, NC])
        nmax_d = sb("nmax_d", [P, NC])
        l_d = sb("l_d", [P, NC, N])
        nlk_d = sb("nlk_d", [P, NC])
        p_d = sb("p_d", [P, NC, N])
        sum_d = sb("sum_d", [P, NC])
        inv_d = ring("inv_d", 2, [P, NC])
        top_d = sb("top_d", [P, NC, TOP])
        rest_d = sb("rest_d", [P, NC, N])
        kept_d = sb("kept_d", [P, NC, N])
        pT_d = sb("pT_d", [P, NC, N])
        u_d = sb("u_d", [P, NC, D3])
        r_d = sb("r_d", [P, NC, D3])
        elu_d = sb("elu_d", [P, NC, D3])
        yless1 = ring("yless1", 2, [P, NC, D])
        out_sb = ring("out_sb", 2, [P, NC, D])

        bank = ctx.enter_context(nc.psum_tensor("bank", [P, 8, 512], F32))

        def tile(op):
            return bank[:, BANKS[op][0], :]

        def halves(op):
            return tile(op).rearrange("p (g n) -> p g n", g=2)

        in_w1, in_w2, in_consts = sem("in_w1"), sem("in_w2"), sem("in_consts")
        in_x_a, in_adjT_a, in_x_c, in_adj_d = sems("in_x_a", 2), sems("in_adjT_a", 2), sems("in_x_c", 2), sems("in_adj_d", 2)
        stored = sems("stored", 2)
        id_zero, id_done, od_done, fills_done = sem("id_zero"), sem("id_done"), sem("od_done"), sem("fills_done")
        parts_zero, parts_done, weights_done = sem("parts_zero"), sem("parts_done"), sem("weights_done")
        w2_sums_mm, w2_sums_done = sem("w2_sums_mm"), sem("w2_sums_done")
        dve_passed, pool_passed = sem("dve_passed"), sem("pool_passed")
        bn_a_done, mv_a_done, stats_a_done, rstd_a_done = sem("bn_a_done"), sem("mv_a_done"), sem("stats_a_done"), sem("rstd_a_done")
        xn_a_done, xnT_a_done, hT_a_done = sem("xn_a_done"), sem("xnT_a_done"), sem("hT_a_done")
        hT_hi_a_done, hT_lo_a_done = sem("hT_hi_a_done"), sem("hT_lo_a_done")
        negT_done = sem("negT_done")
        hi_a_done, parts_a_done, termsT_a_done, terms_a_done = (
            sem("hi_a_done"), sem("parts_a_done"), sem("termsT_a_done"), sem("terms_a_done"))
        xl_mm, xl_done = sems("xl_mm", NC), sems("xl_done", NC)
        t_b_half, t_b_done, e_b_done = sems("t_b_half", NC), sems("t_b_done", NC), sems("e_b_done", NC)
        nmax_b_done, l_b_done, p_b_done = sems("nmax_b_done", NC), sems("l_b_done", NC), sems("p_b_done", NC)
        inv_b_done, pn_b_done = sems("inv_b_done", NC), sems("pn_b_done", NC)
        pT_b_mm, pT_b_done, o_b_mm = sems("pT_b_mm", H), sems("pT_b_done", H), sems("o_b_mm", H)
        u_b_done, h1_done = sems("u_b_done", G), sems("h1_done", G)
        h1_hi_done, h1_lo_done = sems("h1_hi_done", G), sems("h1_lo_done", G)
        xb_c_done = sem("xb_c_done")
        xl_c_mm, xl_c_done = sems("xl_c_mm", NC), sems("xl_c_done", NC)
        hi_c_done, parts_c_done, termsT_c_done, terms_c_done = sem("hi_c_done"), sem("parts_c_done"), sem("termsT_c_done"), sem("terms_c_done")
        t_c_done, e_c_done, nmax_c_done, l_c_done, p_c_done = (
            sem("t_c_done"), sem("e_c_done"), sem("nmax_c_done"), sem("l_c_done"), sem("p_c_done"))
        inv_c_done, pT_c_mm, pT_c_done, o_c_done, y_done = (
            sem("inv_c_done"), sem("pT_c_mm"), sem("pT_c_done"), sem("o_c_done"), sem("y_done"))
        bn_d_done, mv_d_done, stats_d_done, rstd_d_done = sem("bn_d_done"), sem("mv_d_done"), sem("stats_d_done"), sem("rstd_d_done")
        xn_d_done, xnT_d_done, hT_d_done, neg_d_done = sem("xn_d_done"), sem("xnT_d_done"), sem("hT_d_done"), sem("neg_d_done")
        hT_hi_d_done, hT_lo_d_done = sem("hT_hi_d_done"), sem("hT_lo_d_done")
        wh_mm, wh_done = sems("wh_mm", NC), sems("wh_done", NC)
        hi_d_done, parts_d_done, termsT_d_done, terms_d_done = sem("hi_d_done"), sem("parts_d_done"), sem("termsT_d_done"), sem("terms_d_done")
        t_d_done, e_d_done, nmax_d_done, l_d_done, p_d_done = (
            sem("t_d_done"), sem("e_d_done"), sem("nmax_d_done"), sem("l_d_done"), sem("p_d_done"))
        top8_done, rest_done, top16_done, kept_done = sem("top8_done"), sem("rest_done"), sem("top16_done"), sem("kept_done")
        inv_d_done, pT_d_mm, pT_d_done, o_d_done = sem("inv_d_done"), sem("pT_d_mm"), sem("pT_d_done"), sem("o_d_done")
        u_d_done, r_d_done, elu_done, yless1_done, out_done = sem("u_d_done"), sem("r_d_done"), sem("elu_done"), sem("yless1_done"), sem("out_done")

        READ = {
            "xnT_a": hT_hi_a_done, "xl0": xl_done[0], "xl1": xl_done[1], "termsT_a": terms_a_done,
            "t_b": e_b_done[1],
            "pT0_b": pT_b_done[0], "pT1_b": pT_b_done[1], "pT2_b": pT_b_done[2], "pT3_b": pT_b_done[3],
            "o0_b": h1_done[0], "o2_b": h1_done[1],
            "xl0_c": xl_c_done[0], "xl1_c": xl_c_done[1], "termsT_c": terms_c_done, "t_c": e_c_done, "pT_c": pT_c_done, "o_c": y_done,
            "xnT_d": hT_hi_d_done, "wh0_d": wh_done[0], "wh1_d": wh_done[1], "termsT_d": terms_d_done, "t_d": e_d_done,
            "pT_d": pT_d_done, "o_d": r_d_done,
        }

        def bank_free(eng, b, op):
            step = b.k + LAG[op]
            for n in BANKS[op]:
                users = USERS[n]
                me = users.index(op)
                for other in [(me - 1) % len(users)] if b.j is not None else range(len(users)):
                    before = 0 if other < me else 1
                    value = Batch(b.j, step - LAG[users[other]]).count(before)
                    if isinstance(value, int):
                        value = min(value, NB)
                    wait(eng, READ[users[other]], value)

        FIRST = MAX_LAG + 2 + MAX_LAG % 2

        def run(eng, program):
            def step(j, s):
                def do(op, f, *args):
                    k = s - LAG[op]
                    if j is not None or 0 <= k <= LAST:
                        f(Batch(j, k), *args)
                program(do)

            for s in range(FIRST):
                step(None, s)
            with eng.Fori(0, (NB - FIRST) // 2) as j:
                step(j, FIRST)
                step(j, FIRST + 1)
            for s in range(NB, NB + MAX_LAG):
                step(None, s)

        W1_LOADS, CONST_LOADS = 16 * (G * KC + 2), 16 * 7
        W1_WEIGHTS = KC * 2 * H + 3
        B1_WEIGHTS = W1_WEIGHTS + H * 2 + 8
        WEIGHTS = B1_WEIGHTS + KC * 2 + 5

        block = ctx.enter_context(nc.Block())

        def rows(a, b):
            return a[b.index, :, :].rearrange("(c p) d -> p c d", p=P)

        @block.sync
        def _(sp):
            def load(b, dst, src, loaded, read):
                wait(sp, read, b.count(2))
                sp.dma_start(b.of(dst)[:], rows(src, b)).then_inc(b.of(loaded), 16)

            def store(b):
                sp.wait_ge(out_done, b.count())
                sp.dma_start(rows(out, b), b.of(out_sb)[:]).then_inc(b.of(stored), 16)

            def sp_step(do):
                do("load_x_a", load, x_a, x, in_x_a, xn_a_done)
                do("load_x_c", load, x_c, x, in_x_c, xb_c_done)
                do("load_adj_d", load, adj_d, adj, in_adj_d, neg_d_done)
                do("load_adjT_a", load, adjT_a, adj_turned, in_adjT_a, negT_done)
                do("store", store)

            run(sp, sp_step)
            for done in stored:
                sp.wait_ge(done, 16 * NB // 2)


        @block.gpsimd
        def _(pool):
            nc.gpsimd.memset(ident[:], 0.0)
            nc.gpsimd.memset(neg_off_diag[:], NEG).then_inc(id_zero, 1)
            pool.wait_ge(id_zero, 1)
            nc.gpsimd.affine_select(out=ident[:], in_=ident[:], compare_op=ALU.not_equal, fill=1.0, base=0,
                                    pattern=[[-1, P]], channel_multiplier=1).then_inc(id_done, 1)
            nc.gpsimd.affine_select(out=neg_off_diag[:], in_=neg_off_diag[:], compare_op=ALU.not_equal, fill=0.0, base=0,
                                    pattern=[[P, NC], [-1, N]], channel_multiplier=1).then_inc(od_done, 1)
            nc.gpsimd.memset(ones[:], 1.0)
            nc.gpsimd.memset(minus_one[:], -1.0)
            nc.gpsimd.memset(minus_half[:], -0.5).then_inc(fills_done, 1)
            pool.wait_ge(fills_done, 1)

            def rstd(b, veps, dst, stats_done, done, xn_done):
                pool.wait_ge(stats_done, b.count())
                wait(pool, xn_done, b.count(1))
                nc.gpsimd.tensor_tensor(dst[:], veps[:], minus_half[:], ALU.pow).then_inc(done, 1)

            def normalise(b, dst, src, nmean, scale, scale_done, done, turned):
                pool.wait_ge(scale_done, b.count())
                wait(pool, turned, b.count(len(dst)))
                settle(pool, pool_passed)
                for n in range(NC):
                    last = nc.gpsimd.tensor_scalar(b.of(dst)[:, n, :], b.of(src)[:, n, :], nmean[:, n:n + 1],
                                                   scale[:, n:n + 1], ALU.add, ALU.mult)
                last.then_inc(done, 1)

            def make_rstd_a(b):
                rstd(b, veps_a, rstd_a, stats_a_done, rstd_a_done, xn_a_done)

            def make_xn_a(b):
                pool.wait_ge(b.of(in_x_a), b.dma_count())
                normalise(b, xn_a, x_a, nmean_a, rstd_a, rstd_a_done, xn_a_done, xnT_a_done)

            def low(b, dst, full, hi, hi_done, done, mm):
                pool.wait_ge(hi_done, b.count())
                wait(pool, mm, b.count(1))
                nc.gpsimd.tensor_tensor(dst, full, hi.bitcast(F32), ALU.subtract).then_inc(done, 1)

            def make_hT_lo_a(b):
                pool.wait_ge(hT_a_done, b.count())
                low(b, b.of(hT_lo_a)[:], b.of(hT_a)[:], b.of(hT_hi_a)[:], hT_hi_a_done, hT_lo_a_done, xl_mm[LAST_XL])

            def make_hT_lo_d(b):
                pool.wait_ge(hT_d_done, b.count())
                low(b, b.of(hT_lo_d)[:], b.of(hT_d)[:], b.of(hT_hi_d)[:], hT_hi_d_done, hT_lo_d_done, wh_mm[LAST_WH])

            def make_h1_lo_b(b, g):
                h = slice(g * HG, (g + 1) * HG)
                pool.wait_ge(h1_done[g], b.count())
                low(b, h1T_lo[:, h], h1T[:, h], h1T_hi[:, h], h1_hi_done[g], h1_lo_done[g], xl_c_mm[LAST_XL2])

            def make_norm_b(b, n):
                pool.wait_ge(inv_b_done[n], b.count())
                wait(pool, pT_b_mm[LAST_TURNED], b.count(1))
                settle(pool, pool_passed)
                for h in range(H):
                    last = nc.gpsimd.tensor_scalar(pn_b[:, n, h, :], p_b[:, n, h, :], inv_b[:, n, h:h + 1], 1.0,
                                                   ALU.mult, ALU.mult)
                last.then_inc(pn_b_done[n], 1)

            def make_xb_c(b):
                if b.j is None and b.k == 0:
                    pool.wait_ge(weights_done, WEIGHTS)
                pool.wait_ge(b.of(in_x_c), b.dma_count())
                wait(pool, y_done, b.count(len(xb_c)))
                for n in range(NC):
                    last = nc.gpsimd.tensor_tensor(b.of(xb_c)[:, n, :], b.of(x_c)[:, n, :], b2_row[:], ALU.add)
                last.then_inc(xb_c_done, 1)

            def make_rstd_d(b):
                rstd(b, veps_d, rstd_d, stats_d_done, rstd_d_done, xn_d_done)

            def make_xn_d(b):
                normalise(b, xn_d, y, nmean_d, rstd_d, rstd_d_done, xn_d_done, xnT_d_done)

            def make_yless1_d(b):
                pool.wait_ge(y_done, b.count())
                wait(pool, out_done, b.count(len(yless1)))
                settle(pool, pool_passed)
                nc.gpsimd.tensor_scalar(b.of(yless1)[:], b.of(y)[:], -1.0, 1.0, ALU.add, ALU.mult).then_inc(yless1_done, 1)

            def make_add_d(b):
                pool.wait_ge(yless1_done, b.count())
                pool.wait_ge(elu_done, b.count())
                if b.j is not None or b.k >= 2:
                    pool.wait_ge(b.of(stored), b.dma_count(2))
                nc.gpsimd.tensor_tensor(b.of(out_sb)[:], elu_d[:], b.of(yless1)[:], ALU.add).then_inc(out_done, 1)

            def pool_step(do):
                do("h1_lo1_b", make_h1_lo_b, 1)
                do("rstd_a", make_rstd_a)
                do("yless1", make_yless1_d)
                do("xn_a", make_xn_a)
                do("norm1_b", make_norm_b, 1)
                do("norm0_b", make_norm_b, 0)
                do("rstd_d", make_rstd_d)
                do("xn_d", make_xn_d)
                do("xb_c", make_xb_c)
                do("hT_lo_a", make_hT_lo_a)
                do("hT_lo_d", make_hT_lo_d)
                do("add_d", make_add_d)
                do("h1_lo0_b", make_h1_lo_b, 0)

            run(pool, pool_step)

        @block.scalar
        def _(act):
            for g in range(G):
                for k in range(KC):
                    act.dma_start(w1_sb[:, k, g, 0:HG * F], w1[k * P:(k + 1) * P, g * HG * F:(g + 1) * HG * F]).then_inc(in_w1, 16)
            for n, v in enumerate((att_src1, att_dst1)):
                act.dma_start(att1[:, n, :], v.rearrange("(o h) f -> o (h f)", o=1).to_broadcast([P, H * F])).then_inc(in_w1, 16)
            act.dma_start(w2_sb[:, :, 0:D2], w2.rearrange("(k p) n -> p k n", p=P)).then_inc(in_w2, 16)
            act.dma_start(w3_sb[:, :, 0:D3], w3.rearrange("(k p) n -> p k n", p=P)).then_inc(in_consts, 16)
            for n, v in enumerate((att_src2, att_dst2)):
                act.dma_start(att2[:, n, :], v.to_broadcast([P, D2])).then_inc(in_consts, 16)
            for n, half in enumerate((1, 0)):
                act.dma_start(att3[:, n, :], a3[half * D3:(half + 1) * D3, :].rearrange("d o -> o d").to_broadcast([P, D3])).then_inc(in_consts, 16)
            act.dma_start(b2_row[:], b2.rearrange("(o d) -> o d", o=1).to_broadcast([P, D2])).then_inc(in_consts, 16)
            act.dma_start(b1_two[:], b1.rearrange("(o d) -> o d", o=1).to_broadcast([2, H * F])).then_inc(in_consts, 16)
            act.wait_ge(fills_done, 1)
            act.wait_ge(w2_sums_mm, 1)
            nc.scalar.activation(w2_sums[:, 0:D2], bank[:, 0, 0:D2], ACT.Copy).then_inc(w2_sums_done, 1)

            def evacuate(b, dst, src, done, ready, read, slots, func=ACT.Copy):
                act.wait_ge(ready, b.count())
                wait(act, read, b.count(slots))
                nc.scalar.activation(dst, src, func).then_inc(done, 1)

            def exps(b, dst, src, bias, sums, ready, read, done):
                act.wait_ge(ready, b.count())
                wait(act, read, b.count(1))
                for i in range(src.shape[1]):
                    last = nc.scalar.activation(dst[:, i, :], src[:, i, :], ACT.Exp, bias=bias[:, i:i + 1],
                                                accum_out=sums[:, i:i + 1])
                last.then_inc(done, 1)

            def make_hT_a(b):
                evacuate(b, b.of(hT_a)[:], halves("xnT_a"), hT_a_done, xnT_a_done, hT_lo_a_done, len(hT_a), ACT.Relu)

            def make_hT_hi_a(b):
                evacuate(b, b.of(hT_hi_a)[:], halves("xnT_a"), hT_hi_a_done, xnT_a_done, xl_mm[LAST_XL], len(hT_hi_a), ACT.Relu)

            def make_xl_out(b, n):
                first = BANKS[f"xl{n}"][0]
                evacuate(b, b.of(xl)[:, n], bank[:, first:first + G, 0:W1], xl_done[n], xl_mm[n],
                         o_b_mm[LAST_SUMMED], len(xl))

            def make_terms_a(b):
                evacuate(b, b.of(terms_a)[:], halves("termsT_a"), terms_a_done, termsT_a_done, t_b_done[1], len(terms_a))

            def make_p_b(b, n):
                exps(b, p_b[:, n], l_b[:, n], nlk_b[:, n], sum_b[:, n], l_b_done[n], pn_b_done[n], p_b_done[n])

            def make_pT_out(b, h):
                evacuate(b, pT_b[:, h], halves(f"pT{h}_b"), pT_b_done[h], pT_b_mm[h], o_b_mm[h], 1)

            def make_u_b(b, g):
                act.wait_ge(o_b_mm[(g + 1) * HG - 1], b.count())
                wait(act, h1_done[g], b.count(1))
                nc.scalar.activation(u_b[:, g], tile(f"o{g * HG}_b"), ACT.Exp, bias=minus_one[:]).then_inc(u_b_done[g], 1)

            def make_h1_hi_b(b, g):
                h = slice(g * HG, (g + 1) * HG)
                evacuate(b, h1T_hi[:, h], h1T[:, h], h1_hi_done[g], h1_done[g], xl_c_mm[LAST_XL2], 1)

            def make_xl_c_out(b, n):
                evacuate(b, b.of(xl_c)[:, n], tile(f"xl{n}_c")[:, 0:D2 + 2], xl_c_done[n], xl_c_mm[n], o_c_done, len(xl_c))

            def make_terms_c(b):
                evacuate(b, terms_c[:], halves("termsT_c"), terms_c_done, termsT_c_done, t_c_done, 1)

            def make_p_c(b):
                exps(b, p_c, l_c, nlk_c, sum_c, l_c_done, pT_c_mm, p_c_done)

            def make_pT_c_out(b):
                evacuate(b, pT_c[:], halves("pT_c"), pT_c_done, pT_c_mm, o_c_done, 1)

            def make_hT_d(b):
                evacuate(b, b.of(hT_d)[:], halves("xnT_d"), hT_d_done, xnT_d_done, hT_lo_d_done, len(hT_d), ACT.Relu)

            def make_hT_hi_d(b):
                evacuate(b, b.of(hT_hi_d)[:], halves("xnT_d"), hT_hi_d_done, xnT_d_done, wh_mm[LAST_WH], len(hT_hi_d), ACT.Relu)

            def make_wh_out(b, n):
                evacuate(b, b.of(wh)[:, n], tile(f"wh{n}_d")[:, 0:D3 + 2], wh_done[n], wh_mm[n], o_d_done, len(wh))

            def make_terms_d(b):
                evacuate(b, terms_d[:], halves("termsT_d"), terms_d_done, termsT_d_done, t_d_done, 1)

            def make_p_d(b):
                exps(b, p_d, l_d, nlk_d, sum_d, l_d_done, kept_done, p_d_done)

            def make_pT_d_out(b):
                evacuate(b, pT_d[:], halves("pT_d"), pT_d_done, pT_d_mm, o_d_done, 1)

            def make_u_d(b):
                act.wait_ge(o_d_done, b.count())
                act.wait_ge(inv_d_done, b.count())
                wait(act, elu_done, b.count(1))
                for n in range(NC):
                    last = nc.scalar.activation(u_d[:, n, :], halves("o_d")[:, n, :], ACT.Exp, scale=b.of(inv_d)[:, n:n + 1])
                last.then_inc(u_d_done, 1)

            def make_relu_d(b):
                act.wait_ge(o_d_done, b.count())
                act.wait_ge(inv_d_done, b.count())
                wait(act, elu_done, b.count(1))
                for n in range(NC):
                    last = nc.scalar.activation(r_d[:, n, :], halves("o_d")[:, n, :], ACT.Relu, scale=b.of(inv_d)[:, n:n + 1])
                last.then_inc(r_d_done, 1)

            def act_step(do):
                do("p1_b", make_p_b, 1)
                do("p0_b", make_p_b, 0)
                do("xl1_c_out", make_xl_c_out, 1)
                do("relu_d", make_relu_d)
                do("xl0_out", make_xl_out, 0)
                do("xl0_c_out", make_xl_c_out, 0)
                do("terms_d", make_terms_d)
                do("hT_a", make_hT_a)
                do("pT_d_out", make_pT_d_out)
                do("xl1_out", make_xl_out, 1)
                do("terms_c", make_terms_c)
                do("pT0_out", make_pT_out, 0)
                do("pT2_out", make_pT_out, 2)
                do("pT1_out", make_pT_out, 1)
                do("p_d", make_p_d)
                do("terms_a", make_terms_a)
                do("hT_hi_a", make_hT_hi_a)
                do("u0_b", make_u_b, 0)
                do("pT3_out", make_pT_out, 3)
                do("hT_d", make_hT_d)
                do("hT_hi_d", make_hT_hi_d)
                do("p_c", make_p_c)
                do("h1_hi0_b", make_h1_hi_b, 0)
                do("u1_b", make_u_b, 1)
                do("u_d", make_u_d)
                do("pT_c_out", make_pT_c_out)
                do("h1_hi1_b", make_h1_hi_b, 1)
                do("wh1_out", make_wh_out, 1)
                do("wh0_out", make_wh_out, 0)

            run(act, act_step)

        @block.vector
        def _(dve):
            for t in (parts_a, parts_c, parts_d):
                last = nc.vector.memset(t[:].bitcast(F32), 0.0)
            last.then_inc(parts_zero, 1)
            dve.wait_ge(parts_zero, 1)
            for t in (parts_a, parts_c, parts_d):
                g = t[:].rearrange("p c g (h r) -> p c g h r", r=32)
                for k, r in ((0, 2), (0, 3), (1, 0), (1, 1)):
                    last = nc.vector.memset(g[:, :, k, :, r].bitcast(F32), 1.0)
            last.then_inc(parts_done, 1)
            made = 0

            def constant(instruction):
                nonlocal made
                instruction.then_inc(weights_done, 1)
                made += 1
                dve.wait_ge(weights_done, made)

            def column(dst, w, att):
                constant(nc.vector.tensor_tensor_reduce(prod[:, 0:w.shape[1]], w, att, 1.0, 0.0, ALU.mult, ALU.add, dst))

            def high_low(full, hi, lo):
                constant(nc.vector.tensor_copy(hi[:], full))
                constant(nc.vector.tensor_tensor(lo[:], full, hi[:].bitcast(F32), ALU.subtract))

            def make_w1_weights(b):
                if b.j is not None or b.k > 0:
                    return
                dve.wait_ge(in_w1, W1_LOADS)
                for k in range(KC):
                    for g in range(2):
                        for h in range(H):
                            q, i = h // HG, h % HG
                            at = HG * F + g * HG + i
                            column(w1_sb[:, k, q, at:at + 1], w1_sb[:, k, q, i * F:(i + 1) * F], att1[:, g, h * F:(h + 1) * F])
                high_low(w1_sb, w1_hi, w1_lo)
                dve.wait_ge(id_done, 1)
                constant(nc.vector.tensor_copy(ident_r[:], ident[:]))
                dve.wait_ge(od_done, 1)
                dve.wait_ge(fills_done, 1)

            def make_w2_weights(b):
                if b.j is not None or b.k > 0:
                    return
                dve.wait_ge(in_w2, 16)
                dve.wait_ge(in_consts, CONST_LOADS)
                for k in range(H):
                    for g in range(2):
                        column(w2_sb[:, k, D2 + g:D2 + g + 1], w2_sb[:, k, 0:D2], att2[:, g, :])
                high_low(w2_sb, w2_hi, w2_lo)

            def make_b1_parts(b):
                if b.j is not None or b.k > 0:
                    return
                constant(nc.vector.tensor_scalar(b1_two[:], b1_two[:], 1.0, None, ALU.add))
                constant(nc.vector.tensor_copy(b1_hi[:], b1_two[:]))
                constant(nc.vector.tensor_tensor(b1_lo[:], b1_two[:], b1_hi[:].bitcast(F32), ALU.subtract))
                constant(nc.vector.tensor_scalar(b1_hi_or_0[:], b1_hi[:].bitcast(F32), ident[0:2, 0:1], None, ALU.mult))
                constant(nc.vector.scalar_tensor_tensor(b1_parts[:], b1_lo[:], ident[0:2, 1:2], b1_hi_or_0[:], ALU.mult, ALU.add))
                constant(nc.vector.tensor_copy(ones_two[:], ones[0:2, :]))

            def make_w3_weights(b):
                if b.j is not None or b.k > 0:
                    return
                for k in range(KC):
                    for g in range(2):
                        column(w3_sb[:, k, D3 + g:D3 + g + 1], w3_sb[:, k, 0:D3], att3[:, g, :])
                high_low(w3_sb[:], w3_hi, w3_lo)
                dve.wait_ge(w2_sums_done, 1)
                column(w2_sums[:, D2:D2 + 1], w2_sums[:, 0:D2], att2[:, 0, :])
                column(w2_sums[:, D2 + 1:D2 + 2], w2_sums[:, 0:D2], att2[:, 1, :])
                constant(nc.vector.tensor_tensor(b2_row[:], b2_row[:], w2_sums[:, 0:D2], ALU.subtract))

            def bn(b, xin, dst, done):
                wait(dve, done, b.count(1))
                for n in range(NC):
                    last = nc.vector.bn_stats(dst[:, n, :], b.of(xin)[:, n, :])
                last.then_inc(done, 1)

            def aggr(b, src, dst, src_done, done):
                dve.wait_ge(src_done, b.count())
                settle(dve, dve_passed)
                for n in range(NC):
                    last = nc.vector.bn_aggr(dst[:, n, :], src[:, n, :])
                last.then_inc(done, 1)

            def stats(b, mv, nmean, veps, mv_done, done, xn_done):
                dve.wait_ge(mv_done, b.count())
                wait(dve, xn_done, b.count(1))
                nc.vector.tensor_scalar(nmean[:], mv[:, :, 0], -1.0, None, ALU.mult)
                nc.vector.tensor_scalar(veps[:], mv[:, :, 1], EPS, None, ALU.add).then_inc(done, 1)

            def places(dst, heads):
                g = dst[:].rearrange("p c g (h r) -> p c g h r", r=32)
                return g[:, :, 0, 0:heads, 0], g[:, :, 1, 0:heads, 2], g[:, :, 0, 0:heads, 1], g[:, :, 1, 0:heads, 3]

            def scores(b, op, mask, e_t, mx, t_done, l_done, e_done):
                dve.wait_ge(t_done, b.count())
                wait(dve, l_done, b.count(1))
                settle(dve, dve_passed)
                for n in range(NC):
                    last = nc.vector.tensor_tensor_reduce(e_t[:, n, :], halves(op)[:, n, :], mask[:, n, :],
                                                          1.0, LOWEST, ALU.add, ALU.max, mx[:, n:n + 1])
                last.then_inc(e_done, 1)

            def leaky(b, e_t, mx, nmx, nlk, l_t, e_done, nmax_done, p_done, l_done):
                dve.wait_ge(e_done, b.count())
                nc.vector.tensor_scalar(nmx, mx, -1.0, None, ALU.mult).then_inc(nmax_done, 1)
                wait(dve, p_done, b.count(1))
                nc.vector.scalar_tensor_tensor(l_t, e_t, SLOPE, e_t, ALU.mult, ALU.max)
                dve.wait_ge(nmax_done, b.count())
                nc.vector.scalar_tensor_tensor(nlk, mx, -SLOPE, nmx, ALU.mult, ALU.min).then_inc(l_done, 1)

            def make_bn_a(b):
                dve.wait_ge(b.of(in_x_a), b.dma_count())
                bn(b, x_a, bn_a, bn_a_done)

            def make_aggr_a(b):
                aggr(b, bn_a, mv_a, bn_a_done, mv_a_done)

            def make_stats_a(b):
                stats(b, mv_a, nmean_a, veps_a, mv_a_done, stats_a_done, xn_a_done)

            def make_negT(b):
                dve.wait_ge(b.of(in_adjT_a), b.dma_count())
                wait(dve, e_c_done, b.count(len(negT)))
                nc.vector.scalar_tensor_tensor(b.of(negT)[:], b.of(adjT_a)[:], 0.0, neg_off_diag[:], ALU.is_le,
                                               ALU.mult).then_inc(negT_done, 1)

            def make_parts_a(b):
                for n in range(NC):
                    dve.wait_ge(xl_done[n], b.count())
                wait(dve, termsT_a_done, b.count(1))
                hi_col, hi_row, lo_col, lo_row = [
                    t.rearrange("p c (q i) -> p c q i", q=G) for t in places(parts_a, H)]
                col, row = b.of(xl)[:, :, :, HG * F:HG * F + HG], b.of(xl)[:, :, :, HG * F + HG:W1]
                nc.vector.tensor_copy(hi_col, col)
                nc.vector.tensor_copy(hi_row, row).then_inc(hi_a_done, 1)
                dve.wait_ge(hi_a_done, b.count())
                nc.vector.tensor_tensor(lo_col, col, hi_col.bitcast(F32), ALU.subtract)
                nc.vector.tensor_tensor(lo_row, row, hi_row.bitcast(F32), ALU.subtract).then_inc(parts_a_done, 1)

            def make_e_b(b, n):
                dve.wait_ge(negT_done, b.count())
                dve.wait_ge(t_b_done[n], b.count())
                wait(dve, l_b_done[n], b.count(1))
                settle(dve, dve_passed)
                for h in range(H):
                    last = nc.vector.tensor_tensor_reduce(
                        e_b[:, n, h, :], bank[:, BANKS["t_b"][2 * n + h % 2], (h // 2) * N:(h // 2 + 1) * N], b.of(negT)[:, n, :],
                        1.0, LOWEST, ALU.add, ALU.max, max_b[:, n, h:h + 1])
                last.then_inc(e_b_done[n], 1)

            def make_l_b(b, n):
                leaky(b, e_b[:, n], max_b[:, n, :], nmax_b[:, n, :], nlk_b[:, n, :], l_b[:, n],
                      e_b_done[n], nmax_b_done[n], p_b_done[n], l_b_done[n])

            def make_inv_b(b, n):
                dve.wait_ge(p_b_done[n], b.count())
                wait(dve, pn_b_done[n], b.count(1))
                nc.vector.reciprocal(inv_b[:, n, :], sum_b[:, n, :]).then_inc(inv_b_done[n], 1)

            def make_h1_b(b, g):
                dve.wait_ge(u_b_done[g], b.count())
                wait(dve, h1_lo_done[g], b.count(1))
                nc.vector.scalar_tensor_tensor(h1T[:, g * HG:(g + 1) * HG, :].rearrange("p h n -> p (h n)"), u_b[:, g], 1.0,
                                               tile(f"o{g * HG}_b"), ALU.min, ALU.max).then_inc(h1_done[g], 1)

            def make_parts_c(b):
                for n in range(NC):
                    dve.wait_ge(xl_c_done[n], b.count())
                wait(dve, termsT_c_done, b.count(1))
                hi_col, hi_row, lo_col, lo_row = places(parts_c, 1)
                col, row = b.of(xl_c)[:, :, D2:D2 + 1], b.of(xl_c)[:, :, D2 + 1:D2 + 2]
                less_col, less_row = w2_sums[:, D2:D2 + 1], w2_sums[:, D2 + 1:D2 + 2]
                nc.vector.tensor_scalar(hi_col, col, less_col, None, ALU.subtract)
                nc.vector.tensor_scalar(hi_row, row, less_row, None, ALU.subtract).then_inc(hi_c_done, 1)
                dve.wait_ge(hi_c_done, b.count())
                nc.vector.scalar_tensor_tensor(lo_col, col, less_col, hi_col.bitcast(F32), ALU.subtract, ALU.subtract)
                nc.vector.scalar_tensor_tensor(lo_row, row, less_row, hi_row.bitcast(F32), ALU.subtract,
                                               ALU.subtract).then_inc(parts_c_done, 1)

            def make_e_c(b):
                dve.wait_ge(negT_done, b.count())
                scores(b, "t_c", b.of(negT), e_c, max_c, t_c_done, l_c_done, e_c_done)

            def make_l_c(b):
                leaky(b, e_c[:], max_c[:], nmax_c[:], nlk_c[:], l_c[:], e_c_done, nmax_c_done, p_c_done, l_c_done)

            def make_inv_c(b):
                dve.wait_ge(p_c_done, b.count())
                nc.vector.reciprocal(inv_c[:], sum_c[:]).then_inc(inv_c_done, 1)

            def make_y_c(b):
                dve.wait_ge(o_c_done, b.count())
                dve.wait_ge(inv_c_done, b.count())
                dve.wait_ge(xb_c_done, b.count())
                wait(dve, yless1_done, b.count(len(y)))
                for n in range(NC):
                    last = nc.vector.scalar_tensor_tensor(b.of(y)[:, n, :], halves("o_c")[:, n, :],
                                                          inv_c[:, n:n + 1], b.of(xb_c)[:, n, :], ALU.mult, ALU.add)
                last.then_inc(y_done, 1)

            def make_bn_d(b):
                dve.wait_ge(y_done, b.count())
                bn(b, y, bn_d, bn_d_done)

            def make_aggr_d(b):
                aggr(b, bn_d, mv_d, bn_d_done, mv_d_done)

            def make_stats_d(b):
                stats(b, mv_d, nmean_d, veps_d, mv_d_done, stats_d_done, xn_d_done)

            def make_mask_d(b):
                dve.wait_ge(b.of(in_adj_d), b.dma_count())
                wait(dve, e_d_done, b.count(1))
                nc.vector.tensor_scalar(neg_d[:], b.of(adj_d)[:], 0.0, NEG, ALU.is_le, ALU.mult).then_inc(neg_d_done, 1)

            def make_parts_d(b):
                for n in range(NC):
                    dve.wait_ge(wh_done[n], b.count())
                wait(dve, termsT_d_done, b.count(1))
                hi_col, hi_row, lo_col, lo_row = places(parts_d, 1)
                col, row = b.of(wh)[:, :, D3:D3 + 1], b.of(wh)[:, :, D3 + 1:D3 + 2]
                nc.vector.tensor_copy(hi_col, col)
                nc.vector.tensor_copy(hi_row, row).then_inc(hi_d_done, 1)
                dve.wait_ge(hi_d_done, b.count())
                nc.vector.tensor_tensor(lo_col, col, hi_col.bitcast(F32), ALU.subtract)
                nc.vector.tensor_tensor(lo_row, row, hi_row.bitcast(F32), ALU.subtract).then_inc(parts_d_done, 1)

            def make_e_d(b):
                dve.wait_ge(neg_d_done, b.count())
                scores(b, "t_d", neg_d, e_d, max_d, t_d_done, l_d_done, e_d_done)

            def make_l_d(b):
                leaky(b, e_d[:], max_d[:], nmax_d[:], nlk_d[:], l_d[:], e_d_done, nmax_d_done, p_d_done, l_d_done)

            def make_top8_d(b):
                dve.wait_ge(p_d_done, b.count())
                wait(dve, kept_done, b.count(1))
                settle(dve, dve_passed)
                for n in range(NC):
                    last = nc.vector.max(top_d[:, n, 0:8], p_d[:, n, :])
                last.then_inc(top8_done, 1)

            def make_rest_d(b):
                dve.wait_ge(top8_done, b.count())
                settle(dve, dve_passed)
                for n in range(NC):
                    last = nc.vector.match_replace(rest_d[:, n, :], top_d[:, n, 0:8], p_d[:, n, :], -1.0)
                last.then_inc(rest_done, 1)

            def make_top16_d(b):
                dve.wait_ge(rest_done, b.count())
                settle(dve, dve_passed)
                for n in range(NC):
                    last = nc.vector.max(top_d[:, n, 8:16], rest_d[:, n, :])
                last.then_inc(top16_done, 1)
                nc.vector.reciprocal(b.of(inv_d)[:], sum_d[:]).then_inc(inv_d_done, 1)

            def make_kept_d(b):
                dve.wait_ge(top16_done, b.count())
                wait(dve, pT_d_mm, b.count(1))
                for n in range(NC):
                    last = nc.vector.scalar_tensor_tensor(kept_d[:, n, :], p_d[:, n, :], top_d[:, n, TOP - 1:TOP],
                                                          p_d[:, n, :], ALU.is_ge, ALU.mult)
                last.then_inc(kept_done, 1)

            def make_elu_d(b):
                dve.wait_ge(u_d_done, b.count())
                dve.wait_ge(r_d_done, b.count())
                wait(dve, out_done, b.count(1))
                nc.vector.scalar_tensor_tensor(elu_d[:], u_d[:], 1.0, r_d[:], ALU.min, ALU.add).then_inc(elu_done, 1)

            def dve_step(do):
                do("top16_d", make_top16_d)
                do("inv_c", make_inv_c)
                do("inv1_b", make_b1_parts)
                do("inv1_b", make_inv_b, 1)
                do("kept_d", make_kept_d)
                do("parts_d", make_parts_d)
                do("y_c", make_y_c)
                do("inv0_b", make_inv_b, 0)
                do("bn_d", make_bn_d)
                do("mask_d", make_mask_d)
                do("aggr_d", make_aggr_d)
                do("parts_c", make_w3_weights)
                do("parts_c", make_parts_c)
                do("bn_a", make_bn_a)
                do("stats_d", make_stats_d)
                do("e_d", make_e_d)
                do("parts_a", make_w2_weights)
                do("parts_a", make_parts_a)
                do("l_d", make_l_d)
                do("e_c", make_e_c)
                do("aggr_a", make_aggr_a)
                do("l_c", make_l_c)
                do("elu_d", make_elu_d)
                do("top8_d", make_top8_d)
                do("negT", make_negT)
                do("h1_0_b", make_h1_b, 0)
                do("e0_b", make_e_b, 0)
                do("e1_b", make_e_b, 1)
                do("h1_1_b", make_h1_b, 1)
                do("l1_b", make_l_b, 1)
                do("stats_a", make_stats_a)
                do("stats_a", make_w1_weights)
                do("rest_d", make_rest_d)
                do("l0_b", make_l_b, 0)

            run(dve, dve_step)

        @block.tensor
        def _(pe):
            pe.wait_ge(id_done, 1)
            pe.wait_ge(fills_done, 1)
            pe.wait_ge(in_w2, 16)
            for k in range(H):
                last = nc.tensor.matmul(bank[:, 0, 0:D2], ones[:, 0:P], w2_sb[:, k, 0:D2], start=(k == 0), stop=(k == H - 1))
            last.then_inc(w2_sums_mm, 1)
            pe.wait_ge(w2_sums_done, 1)

            def turn(dst, src):
                for k in range(2):
                    for n in range(2):
                        last = nc.tensor.transpose(dst[:, k, n * P:(n + 1) * P], src[:, n, k * P:(k + 1) * P], ident[:])
                return last

            def terms(b, op, src, ready, done):
                pe.wait_ge(ready, b.count())
                bank_free(pe, b, op)
                for n in range(NC):
                    for g in range(2):
                        last = nc.tensor.transpose(halves(op)[:, g, n * P:(n + 1) * P].bitcast(F32R), src[:, n, g, :], ident_r[:])
                last.then_inc(done, 1)

            def project(dst, hi, lo, w_hi, w_lo, n):
                K = w_hi.shape[1]
                passes = [(a, w, k) for k in range(K) for a, w in ((hi, w_hi), (hi, w_lo), (lo, w_hi))]
                for i, (a, w, k) in enumerate(passes):
                    last = nc.tensor.matmul(dst, a[:, k, n * P:(n + 1) * P], w[:, k], start=(i == 0), stop=(i == len(passes) - 1))
                return last

            def t_one(b, op, src, ready, done):
                pe.wait_ge(ready, b.count())
                bank_free(pe, b, op)
                for n in range(NC):
                    last = nc.tensor.matmul(halves(op)[:, n, :], src[0:4, 1, n * P:(n + 1) * P], src[0:4, 0, :],
                                            start=True, stop=True)
                last.then_inc(done, 1)

            def attend(b, op, pT, feats, ready, done):
                pe.wait_ge(ready, b.count())
                bank_free(pe, b, op)
                for n in range(NC):
                    for k in range(NC):
                        last = nc.tensor.matmul(halves(op)[:, n, :], pT[:, k, n * P:(n + 1) * P], feats[:, k, 0:D2],
                                                start=(k == 0), stop=(k == NC - 1))
                last.then_inc(done, 1)

            def make_xnT_a(b):
                pe.wait_ge(xn_a_done, b.count())
                bank_free(pe, b, "xnT_a")
                turn(halves("xnT_a"), b.of(xn_a)).then_inc(xnT_a_done, 1)

            def make_project_a(b, n):
                pe.wait_ge(hT_hi_a_done, b.count())
                pe.wait_ge(hT_lo_a_done, b.count())
                if b.j is None and b.k == 0:
                    pe.wait_ge(weights_done, W1_WEIGHTS)
                bank_free(pe, b, f"xl{n}")
                for g in range(G):
                    last = project(bank[:, BANKS[f"xl{n}"][g], 0:W1], b.of(hT_hi_a), b.of(hT_lo_a),
                                         w1_hi[:, :, g, :], w1_lo[:, :, g, :], n)
                last.then_inc(xl_mm[n], 1)

            def make_termsT_a(b):
                terms(b, "termsT_a", parts_a, parts_a_done, termsT_a_done)

            def make_t_b(b):
                pe.wait_ge(terms_a_done, b.count())
                bank_free(pe, b, "t_b")
                for half in range(2):
                    for n in range(NC):
                        if half == 1:
                            pe.wait_ge(t_b_half[n], b.count())
                        for i in range(2):
                            r = slice(32 * (2 * half + i), 32 * (2 * half + i) + 4)
                            last = nc.tensor.matmul(bank[:, BANKS["t_b"][2 * n + i], half * N:(half + 1) * N],
                                                    b.of(terms_a)[r, 1, n * P:(n + 1) * P], b.of(terms_a)[r, 0, :],
                                                    start=True, stop=True)
                        last.then_inc((t_b_half if half == 0 else t_b_done)[n], 1)

            def make_pT_b(b, h):
                for n in range(NC):
                    pe.wait_ge(pn_b_done[n], b.count())
                bank_free(pe, b, f"pT{h}_b")
                turn(halves(f"pT{h}_b"), pn_b[:, :, h, :]).then_inc(pT_b_mm[h], 1)

            def make_o_b(b, h):
                g, i = h // HG, h % HG
                if i == 0:
                    bank_free(pe, b, f"o{h}_b")
                if b.j is None and b.k == 0:
                    pe.wait_ge(weights_done, B1_WEIGHTS)
                dst = tile(f"o{g * HG}_b")[:, i * N:(i + 1) * N]
                pe.wait_ge(pT_b_done[h], b.count())
                for n in range(NC):
                    pe.wait_ge(xl_done[n], b.count())
                nc.tensor.matmul(dst, b1_parts[:, h * F:(h + 1) * F], ones_two[:], start=True, stop=False)
                for k in range(NC):
                    last = nc.tensor.matmul(dst, b.of(xl)[:, k, g, i * F:(i + 1) * F], pT_b[:, h, k, :],
                                            start=False, stop=(k == NC - 1))
                last.then_inc(o_b_mm[h], 1)

            def make_project_c(b, n):
                for g in range(G):
                    pe.wait_ge(h1_hi_done[g], b.count())
                    pe.wait_ge(h1_lo_done[g], b.count())
                bank_free(pe, b, f"xl{n}_c")
                project(tile(f"xl{n}_c")[:, 0:D2 + 2], h1T_hi, h1T_lo, w2_hi, w2_lo, n).then_inc(xl_c_mm[n], 1)

            def make_termsT_c(b):
                terms(b, "termsT_c", parts_c, parts_c_done, termsT_c_done)

            def make_t_c(b):
                t_one(b, "t_c", terms_c, terms_c_done, t_c_done)

            def make_pT_c(b):
                pe.wait_ge(p_c_done, b.count())
                bank_free(pe, b, "pT_c")
                turn(halves("pT_c"), p_c).then_inc(pT_c_mm, 1)

            def make_o_c(b):
                attend(b, "o_c", pT_c, b.of(xl_c), pT_c_done, o_c_done)

            def make_xnT_d(b):
                pe.wait_ge(xn_d_done, b.count())
                bank_free(pe, b, "xnT_d")
                turn(halves("xnT_d"), b.of(xn_d)).then_inc(xnT_d_done, 1)

            def make_project_d(b, n):
                pe.wait_ge(hT_hi_d_done, b.count())
                pe.wait_ge(hT_lo_d_done, b.count())
                if b.j is None and b.k == 0:
                    pe.wait_ge(weights_done, WEIGHTS)
                bank_free(pe, b, f"wh{n}_d")
                project(tile(f"wh{n}_d")[:, 0:D3 + 2], b.of(hT_hi_d), b.of(hT_lo_d), w3_hi, w3_lo, n).then_inc(wh_mm[n], 1)

            def make_termsT_d(b):
                terms(b, "termsT_d", parts_d, parts_d_done, termsT_d_done)

            def make_t_d(b):
                t_one(b, "t_d", terms_d, terms_d_done, t_d_done)

            def make_pT_d(b):
                pe.wait_ge(kept_done, b.count())
                bank_free(pe, b, "pT_d")
                turn(halves("pT_d"), kept_d).then_inc(pT_d_mm, 1)

            def make_o_d(b):
                attend(b, "o_d", pT_d, b.of(wh), pT_d_done, o_d_done)

            def pe_step(do):
                do("t_d", make_t_d)
                do("termsT_c", make_termsT_c)
                do("pT0_b", make_pT_b, 0)
                do("pT2_b", make_pT_b, 2)
                do("pT1_b", make_pT_b, 1)
                do("t_c", make_t_c)
                do("o0_b", make_o_b, 0)
                do("termsT_a", make_termsT_a)
                do("o1_b", make_o_b, 1)
                do("xnT_d", make_xnT_d)
                do("pT3_b", make_pT_b, 3)
                do("t_b", make_t_b)
                do("o2_b", make_o_b, 2)
                do("o3_b", make_o_b, 3)
                do("o_d", make_o_d)
                do("pT_c", make_pT_c)
                do("wh1_d", make_project_d, 1)
                do("wh0_d", make_project_d, 0)
                do("o_c", make_o_c)
                do("xl0", make_project_a, 0)
                do("xl1_c", make_project_c, 1)
                do("xl0_c", make_project_c, 0)
                do("xnT_a", make_xnT_a)
                do("termsT_d", make_termsT_d)
                do("pT_d", make_pT_d)
                do("xl1", make_project_a, 1)

            run(pe, pe_step)


_INS = ["x", "adj", "L0_gnn_W1", "L0_gnn_att_src1", "L0_gnn_att_dst1", "L0_gnn_b1", "L0_gnn_W2",
        "L0_gnn_att_src2", "L0_gnn_att_dst2", "L0_gnn_b2", "L1_gnn_W", "L1_gnn_a"]


def kernel(**inputs):
    import numpy as _np
    import concourse.bacc as _bacc
    from concourse import mybir as _mybir
    from concourse.bass_utils import run_bass_kernel_spmd as _run

    nc = _bacc.Bacc("TRN2", target_bir_lowering=False, num_devices=1)
    arrays, args = {}, []
    for name in _INS:
        a = _np.ascontiguousarray(inputs[name])
        arrays[f"in_{name}"] = a
        args.append(nc.dram_tensor(f"in_{name}", a.shape, _mybir.dt.from_np(a.dtype), kind="ExternalInput").ap())
    a = _np.ascontiguousarray(_np.swapaxes(inputs["adj"], 1, 2))
    arrays["in_adj_turned"] = a
    args.insert(2, nc.dram_tensor("in_adj_turned", a.shape, _mybir.dt.from_np(a.dtype), kind="ExternalInput").ap())
    shape = inputs["x"].shape
    args.append(nc.dram_tensor("out_x", shape, _mybir.dt.float32, kind="ExternalOutput").ap())
    gat_stack(nc, *args)
    r = _run(nc, [arrays], core_ids=[0])
    return r.results[0]["out_x"]
```
